# Optimizing a Trainium2 kernel written in Bass

```python
import numpy as np
import jax
import jax.numpy as jnp

def _softmax(x, axis=-1):
    return jax.nn.softmax(x, axis=axis)

def _gelu(x):
    return jax.nn.gelu(x, approximate=True)

def _silu(x):
    return jax.nn.silu(x)

def _sigmoid(x):
    return jax.nn.sigmoid(x)

def _layernorm(x, axis=-1, eps=1e-05):
    m = jnp.mean(x, axis=axis, keepdims=True)
    v = jnp.var(x, axis=axis, keepdims=True)
    return (x - m) / jnp.sqrt(v + eps)

def _scatter_add(tgt, idx, src, axis=0):
    return tgt.at[idx].add(src)

def _segment_sum(src, seg, n):
    return jax.ops.segment_sum(src, seg, n)
kernel_name = 'mk_prb_d4_jaxref_r4_454133'

def setup_inputs(seed: int=0):
    np.random.seed(seed)
    _w = jnp.asarray

    def _L0_attn_setup():
        import jax, jax.numpy as jnp
        import numpy as np
        HEADS = 4
        EPS = 1e-05
        GATE_LOGIT_NORMALIZER = 16.0
        B, N, D = (4, 512, 256)
        DK, DV, R = (256, 512, 16)

        def _gla_scan(q, k, v, gk):
            dk, dv = (q.shape[1], v.shape[1])

            def step(S, inp):
                q_t, k_t, v_t, g_t = inp
                S = S * jnp.exp(g_t)[:, None] + k_t[:, None] * v_t[None, :]
                return (S, q_t @ S)
            S0 = jnp.zeros((dk, dv), q.dtype)
            _, o = jax.lax.scan(step, S0, (q, k, v, gk))
            return o
        key = jax.random.key(seed)
        ks = jax.random.split(key, 10)
        s = 0.02
        return {'x': jax.random.normal(ks[0], (B, N, D), jnp.float32), 'Wq': jax.random.normal(ks[1], (D, DK), jnp.float32) * s, 'Wk': jax.random.normal(ks[2], (D, DK), jnp.float32) * s, 'Wv': jax.random.normal(ks[3], (D, DV), jnp.float32) * s, 'Wg': jax.random.normal(ks[4], (D, DV), jnp.float32) * s, 'Wgk1': jax.random.normal(ks[5], (D, R), jnp.float32) * s, 'Wgk2': jax.random.normal(ks[6], (R, DK), jnp.float32) * s, 'bgk2': jnp.zeros((DK,), jnp.float32), 'Wo': jax.random.normal(ks[7], (DV, D), jnp.float32) * s, 'g_norm_weight': jnp.ones((DV // HEADS,), jnp.float32)}
    _L0_attn_in = _L0_attn_setup()

    def _L0_ffn_setup():
        import jax, jax.numpy as jnp
        import numpy as np
        DIM = 256
        NUM_EXPERTS = 8
        TOP_K = 2
        HIDDEN = int(DIM * 1.5)
        key = jax.random.key(seed)
        k_x, k_r, k_w1, k_w2, k_w3 = jax.random.split(key, 5)
        B, T = (2, 1024)
        s_in = 1.0 / np.sqrt(DIM)
        s_h = 1.0 / np.sqrt(HIDDEN)
        return {'x': jax.random.normal(k_x, (B, T, DIM), dtype=jnp.float32), 'Wr': jax.random.uniform(k_r, (DIM, NUM_EXPERTS), minval=-s_in, maxval=s_in, dtype=jnp.float32), 'W1': jax.random.uniform(k_w1, (NUM_EXPERTS, DIM, HIDDEN), minval=-s_in, maxval=s_in, dtype=jnp.float32), 'W2': jax.random.uniform(k_w2, (NUM_EXPERTS, HIDDEN, DIM), minval=-s_h, maxval=s_h, dtype=jnp.float32), 'W3': jax.random.uniform(k_w3, (NUM_EXPERTS, DIM, HIDDEN), minval=-s_in, maxval=s_in, dtype=jnp.float32)}
    _L0_ffn_in = _L0_ffn_setup()

    def _L1_attn_setup():
        import jax, jax.numpy as jnp
        import numpy as np
        B_SZ, L, D_MODEL = (2, 512, 256)
        EXPAND, N_STATE, K = (2, 16, 4)
        D_INNER = D_MODEL * EXPAND

        def _layernorm(x, g, b, eps=1e-05):
            mu = jnp.mean(x, axis=-1, keepdims=True)
            var = jnp.var(x, axis=-1, keepdims=True)
            return (x - mu) * jax.lax.rsqrt(var + eps) * g + b

        def _selective_scan(x, delta, A, B_mat, C_mat, D_vec):
            dA = jnp.exp(delta[..., None] * A)
            Bx = jnp.einsum('bld,nd->bln', x, B_mat) * delta[..., None]

            def step(h, inp):
                dA_t, Bx_t = inp
                h = dA_t * h + Bx_t
                return (h, h)
            h0 = jnp.zeros((x.shape[0], A.shape[0]), x.dtype)
            _, hs = jax.lax.scan(step, h0, (jnp.swapaxes(dA, 0, 1), jnp.swapaxes(Bx, 0, 1)))
            hs = jnp.swapaxes(hs, 0, 1)
            return jnp.einsum('bln,dn->bld', hs, C_mat) + D_vec * x
        key = jax.random.key(seed)
        ks = jax.random.split(key, 12)
        s = lambda k, shape, scale=0.02: jax.random.normal(k, shape, jnp.float32) * scale
        return {'x': jax.random.normal(ks[0], (B_SZ, L, D_MODEL), jnp.float32), 'ln_gamma': jnp.ones((D_MODEL,), jnp.float32), 'ln_beta': jnp.zeros((D_MODEL,), jnp.float32), 'W_in': s(ks[1], (D_MODEL, 2 * D_INNER)), 'conv_w': s(ks[2], (D_INNER, 1, K), 0.1), 'conv_b': jnp.zeros((D_INNER,), jnp.float32), 'A_log': jax.random.normal(ks[3], (N_STATE,), jnp.float32), 'B_mat': s(ks[4], (N_STATE, D_INNER), 0.05), 'C_mat': s(ks[5], (D_INNER, N_STATE), 0.05), 'D_vec': s(ks[6], (D_INNER,), 0.1), 'Wd': s(ks[7], (D_INNER, D_INNER)), 'bd': jnp.zeros((D_INNER,), jnp.float32), 'W_out': s(ks[8], (D_INNER, D_MODEL))}
    _L1_attn_in = _L1_attn_setup()

    def _L1_ffn_setup():
        import jax, jax.numpy as jnp
        import numpy as np
        from jax import lax
        B, N, DIM = (4, 512, 256)
        HEADS = 8
        NUM_EXPERTS = 4096
        NUM_KEYS = 128
        DIM_KEY = DIM // 2
        DIM_INNER = 2 * DIM
        PK_TOPK = 16
        TOPK = 1
        key = jax.random.key(seed)
        ks = jax.random.split(key, 10)
        s = lambda k, shape, std=0.02: jax.random.normal(k, shape, dtype=jnp.float32) * std
        return {'x': jax.random.normal(ks[0], (B, N, DIM), dtype=jnp.float32), 'Wq': s(ks[1], (DIM_KEY * HEADS * 2, DIM)), 'keys': s(ks[2], (HEADS, NUM_KEYS, 2, DIM_KEY)), 'W_in': s(ks[3], (DIM_INNER, DIM)), 'W_out': s(ks[4], (DIM, DIM_INNER)), 'in_a': s(ks[5], (NUM_EXPERTS, DIM)), 'in_b': s(ks[6], (NUM_EXPERTS, DIM_INNER)), 'out_a': s(ks[7], (NUM_EXPERTS, DIM_INNER)), 'out_b': s(ks[8], (NUM_EXPERTS, DIM))}
    _L1_ffn_in = _L1_ffn_setup()

    def _L2_attn_setup():
        import jax, jax.numpy as jnp
        import numpy as np
        H = 256
        F = 1024
        B, S = (4, 1024)
        EPS = 1e-05

        def _layernorm(x, scale, bias):
            mu = jnp.mean(x, axis=-1, keepdims=True)
            var = jnp.var(x, axis=-1, keepdims=True)
            return (x - mu) * jax.lax.rsqrt(var + EPS) * scale + bias
        key = jax.random.key(seed)
        ks = jax.random.split(key, 4)
        x = jax.random.normal(ks[0], (B, S, H), dtype=jnp.float32)
        W_ret = jax.random.normal(ks[1], (H, H), dtype=jnp.float32) * 0.02
        b_ret = jnp.zeros((H,), dtype=jnp.float32)
        ln1_scale = jnp.ones((H,), dtype=jnp.float32)
        ln1_bias = jnp.zeros((H,), dtype=jnp.float32)
        W1 = jax.random.normal(ks[2], (H, F), dtype=jnp.float32) * 0.02
        b1 = jnp.zeros((F,), dtype=jnp.float32)
        W2 = jax.random.normal(ks[3], (F, H), dtype=jnp.float32) * 0.02
        b2 = jnp.zeros((H,), dtype=jnp.float32)
        ln2_scale = jnp.ones((H,), dtype=jnp.float32)
        ln2_bias = jnp.zeros((H,), dtype=jnp.float32)
        return {'x': x, 'W_ret': W_ret, 'b_ret': b_ret, 'ln1_scale': ln1_scale, 'ln1_bias': ln1_bias, 'W1': W1, 'b1': b1, 'W2': W2, 'b2': b2, 'ln2_scale': ln2_scale, 'ln2_bias': ln2_bias}
    _L2_attn_in = _L2_attn_setup()

    def _L2_ffn_setup():
        import jax, jax.numpy as jnp
        import numpy as np
        import math
        D_IN = 256
        FEATURES = (1024, 1024, 256)
        BATCH, SEQ = (8, 512)

        def _conn_dense(kernel_bool, x):
            w = jnp.where(kernel_bool, jnp.float32(1.0), jnp.float32(-1.0))
            return x @ w
        key = jax.random.key(seed)
        kx, kk0, kk1, kk2 = jax.random.split(key, 4)
        x = jax.random.normal(kx, (BATCH, SEQ, D_IN), dtype=jnp.float32)
        k0 = jax.random.randint(kk0, (2 * D_IN, FEATURES[0]), 0, 2).astype(jnp.bool_)
        k1 = jax.random.randint(kk1, (FEATURES[0], FEATURES[1]), 0, 2).astype(jnp.bool_)
        k2 = jax.random.randint(kk2, (FEATURES[1], FEATURES[2]), 0, 2).astype(jnp.bool_)
        s0 = jnp.asarray(1.0 / math.sqrt(2 * D_IN), dtype=jnp.float32)
        s1 = jnp.asarray(1.0 / math.sqrt(FEATURES[0]), dtype=jnp.float32)
        s2 = jnp.asarray(1.0 / math.sqrt(FEATURES[1]), dtype=jnp.float32)
        return {'x': x, 'k0': k0, 'k1': k1, 'k2': k2, 's0': s0, 's1': s1, 's2': s2}
    _L2_ffn_in = _L2_ffn_setup()

    def _L3_attn_setup():
        import jax, jax.numpy as jnp
        import numpy as np
        key = jax.random.key(seed)
        ks = jax.random.split(key, 5)
        B, S, D = (2, 512, 256)
        scale = 0.02
        return {'x': jax.random.normal(ks[0], (B, S, D), dtype=jnp.float32), 'q_proj_weight': jax.random.normal(ks[1], (D, D), dtype=jnp.float32) * scale, 'k_proj_weight': jax.random.normal(ks[2], (D, D), dtype=jnp.float32) * scale, 'v_proj_weight': jax.random.normal(ks[3], (D, D), dtype=jnp.float32) * scale, 'o_proj_weight': jax.random.normal(ks[4], (D, D), dtype=jnp.float32) * scale}
    _L3_attn_in = _L3_attn_setup()

    def _L3_ffn_setup():
        import jax, jax.numpy as jnp
        import numpy as np
        INPUT_SIZE = 256
        OUTPUT_SIZE = 256
        key = jax.random.key(seed)
        kx, kt, kp, ktn, kpn = jax.random.split(key, 5)
        x = jax.random.normal(kx, (8, 512, INPUT_SIZE), dtype=jnp.float32)
        theta = jax.random.normal(kt, (INPUT_SIZE, OUTPUT_SIZE), dtype=jnp.float32) * 0.02
        phi = jax.random.normal(kp, (INPUT_SIZE, OUTPUT_SIZE), dtype=jnp.float32) * 0.02
        theta_noise = jax.random.normal(ktn, (INPUT_SIZE, OUTPUT_SIZE), dtype=jnp.float32) * 0.01
        phi_noise = jax.random.normal(kpn, (INPUT_SIZE, OUTPUT_SIZE), dtype=jnp.float32) * 0.01
        return {'x': x, 'theta': theta, 'phi': phi, 'theta_noise': theta_noise, 'phi_noise': phi_noise}
    _L3_ffn_in = _L3_ffn_setup()
    _d = {'L0_attn_x': _L0_attn_in['x'], 'L0_attn_Wq': _L0_attn_in['Wq'], 'L0_attn_Wk': _L0_attn_in['Wk'], 'L0_attn_Wv': _L0_attn_in['Wv'], 'L0_attn_Wg': _L0_attn_in['Wg'], 'L0_attn_Wgk1': _L0_attn_in['Wgk1'], 'L0_attn_Wgk2': _L0_attn_in['Wgk2'], 'L0_attn_bgk2': _L0_attn_in['bgk2'], 'L0_attn_Wo': _L0_attn_in['Wo'], 'L0_attn_g_norm_weight': _L0_attn_in['g_norm_weight'], 'L0_ffn_Wr': _L0_ffn_in['Wr'], 'L0_ffn_W1': _L0_ffn_in['W1'], 'L0_ffn_W2': _L0_ffn_in['W2'], 'L0_ffn_W3': _L0_ffn_in['W3'], 'L1_attn_ln_gamma': _L1_attn_in['ln_gamma'], 'L1_attn_ln_beta': _L1_attn_in['ln_beta'], 'L1_attn_W_in': _L1_attn_in['W_in'], 'L1_attn_conv_w': _L1_attn_in['conv_w'], 'L1_attn_conv_b': _L1_attn_in['conv_b'], 'L1_attn_A_log': _L1_attn_in['A_log'], 'L1_attn_B_mat': _L1_attn_in['B_mat'], 'L1_attn_C_mat': _L1_attn_in['C_mat'], 'L1_attn_D_vec': _L1_attn_in['D_vec'], 'L1_attn_Wd': _L1_attn_in['Wd'], 'L1_attn_bd': _L1_attn_in['bd'], 'L1_attn_W_out': _L1_attn_in['W_out'], 'L1_ffn_Wq': _L1_ffn_in['Wq'], 'L1_ffn_keys': _L1_ffn_in['keys'], 'L1_ffn_W_in': _L1_ffn_in['W_in'], 'L1_ffn_W_out': _L1_ffn_in['W_out'], 'L1_ffn_in_a': _L1_ffn_in['in_a'], 'L1_ffn_in_b': _L1_ffn_in['in_b'], 'L1_ffn_out_a': _L1_ffn_in['out_a'], 'L1_ffn_out_b': _L1_ffn_in['out_b'], 'L2_attn_W_ret': _L2_attn_in['W_ret'], 'L2_attn_b_ret': _L2_attn_in['b_ret'], 'L2_attn_ln1_scale': _L2_attn_in['ln1_scale'], 'L2_attn_ln1_bias': _L2_attn_in['ln1_bias'], 'L2_attn_W1': _L2_attn_in['W1'], 'L2_attn_b1': _L2_attn_in['b1'], 'L2_attn_W2': _L2_attn_in['W2'], 'L2_attn_b2': _L2_attn_in['b2'], 'L2_attn_ln2_scale': _L2_attn_in['ln2_scale'], 'L2_attn_ln2_bias': _L2_attn_in['ln2_bias'], 'L2_ffn_k0': _L2_ffn_in['k0'], 'L2_ffn_k1': _L2_ffn_in['k1'], 'L2_ffn_k2': _L2_ffn_in['k2'], 'L2_ffn_s0': _L2_ffn_in['s0'], 'L2_ffn_s1': _L2_ffn_in['s1'], 'L2_ffn_s2': _L2_ffn_in['s2'], 'L3_attn_q_proj_weight': _L3_attn_in['q_proj_weight'], 'L3_attn_k_proj_weight': _L3_attn_in['k_proj_weight'], 'L3_attn_v_proj_weight': _L3_attn_in['v_proj_weight'], 'L3_attn_o_proj_weight': _L3_attn_in['o_proj_weight'], 'L3_ffn_theta': _L3_ffn_in['theta'], 'L3_ffn_phi': _L3_ffn_in['phi'], 'L3_ffn_theta_noise': _L3_ffn_in['theta_noise'], 'L3_ffn_phi_noise': _L3_ffn_in['phi_noise']}
    _x0 = _d['L0_attn_x']
    _d['L0_attn_x'] = jax.random.normal(jax.random.fold_in(jax.random.key(seed), 1), (2, 2048, 256), dtype=_x0.dtype)
    del _x0
    return _d

def reference(L0_attn_x, L0_attn_Wq, L0_attn_Wk, L0_attn_Wv, L0_attn_Wg, L0_attn_Wgk1, L0_attn_Wgk2, L0_attn_bgk2, L0_attn_Wo, L0_attn_g_norm_weight, L0_ffn_Wr, L0_ffn_W1, L0_ffn_W2, L0_ffn_W3, L1_attn_ln_gamma, L1_attn_ln_beta, L1_attn_W_in, L1_attn_conv_w, L1_attn_conv_b, L1_attn_A_log, L1_attn_B_mat, L1_attn_C_mat, L1_attn_D_vec, L1_attn_Wd, L1_attn_bd, L1_attn_W_out, L1_ffn_Wq, L1_ffn_keys, L1_ffn_W_in, L1_ffn_W_out, L1_ffn_in_a, L1_ffn_in_b, L1_ffn_out_a, L1_ffn_out_b, L2_attn_W_ret, L2_attn_b_ret, L2_attn_ln1_scale, L2_attn_ln1_bias, L2_attn_W1, L2_attn_b1, L2_attn_W2, L2_attn_b2, L2_attn_ln2_scale, L2_attn_ln2_bias, L2_ffn_k0, L2_ffn_k1, L2_ffn_k2, L2_ffn_s0, L2_ffn_s1, L2_ffn_s2, L3_attn_q_proj_weight, L3_attn_k_proj_weight, L3_attn_v_proj_weight, L3_attn_o_proj_weight, L3_ffn_theta, L3_ffn_phi, L3_ffn_theta_noise, L3_ffn_phi_noise):

    def _L0_attn_ref(x, Wq, Wk, Wv, Wg, Wgk1, Wgk2, bgk2, Wo, g_norm_weight):
        import jax, jax.numpy as jnp
        import numpy as np
        HEADS = 4
        EPS = 1e-05
        GATE_LOGIT_NORMALIZER = 16.0
        B, N, D = (4, 512, 256)
        DK, DV, R = (256, 512, 16)

        def _gla_scan(q, k, v, gk):
            dk, dv = (q.shape[1], v.shape[1])

            def step(S, inp):
                q_t, k_t, v_t, g_t = inp
                S = S * jnp.exp(g_t)[:, None] + k_t[:, None] * v_t[None, :]
                return (S, q_t @ S)
            S0 = jnp.zeros((dk, dv), q.dtype)
            _, o = jax.lax.scan(step, S0, (q, k, v, gk))
            return o
        b, n, d = x.shape
        h = HEADS
        dk = Wq.shape[1] // h
        dv = Wv.shape[1] // h
        split = lambda t, hd: t.reshape(b, n, h, hd).transpose(0, 2, 1, 3)
        q = split(x @ Wq, dk) * dk ** (-0.5)
        k = split(x @ Wk, dk)
        v = split(x @ Wv, dv)
        gk = jax.nn.log_sigmoid(x @ Wgk1 @ Wgk2 + bgk2) / GATE_LOGIT_NORMALIZER
        gk = split(gk, dk)
        o = jax.vmap(jax.vmap(_gla_scan))(q, k, v, gk)
        o = o.transpose(0, 2, 1, 3)
        g = (x @ Wg).reshape(b, n, h, dv)
        o = o * jax.lax.rsqrt(jnp.mean(o * o, axis=-1, keepdims=True) + EPS) * g_norm_weight
        o = o * (g * jax.nn.sigmoid(g))
        return o.reshape(b, n, h * dv) @ Wo

    def _L0_ffn_ref(x, Wr, W1, W2, W3):
        import jax, jax.numpy as jnp
        import numpy as np
        DIM = 256
        NUM_EXPERTS = 8
        TOP_K = 2
        HIDDEN = int(DIM * 1.5)
        B, T, C = x.shape
        xf = x.reshape(-1, C)
        gate_logits = xf @ Wr
        w, idx = jax.lax.top_k(gate_logits, TOP_K)
        w = jax.nn.softmax(w, axis=-1)
        comb = jnp.sum(w[:, :, None] * jax.nn.one_hot(idx, NUM_EXPERTS, dtype=w.dtype), axis=1)
        h = jnp.einsum('nc,ech->neh', xf, W1)
        g = jnp.einsum('nc,ech->neh', xf, W3)
        y = jnp.einsum('neh,ehc->nec', jax.nn.silu(h) * g, W2)
        out = jnp.einsum('nec,ne->nc', y, comb)
        return out.reshape(B, T, C)

    def _L1_attn_ref(x, ln_gamma, ln_beta, W_in, conv_w, conv_b, A_log, B_mat, C_mat, D_vec, Wd, bd, W_out):
        import jax, jax.numpy as jnp
        import numpy as np
        B_SZ, L, D_MODEL = (2, 512, 256)
        EXPAND, N_STATE, K = (2, 16, 4)
        D_INNER = D_MODEL * EXPAND

        def _layernorm(x, g, b, eps=1e-05):
            mu = jnp.mean(x, axis=-1, keepdims=True)
            var = jnp.var(x, axis=-1, keepdims=True)
            return (x - mu) * jax.lax.rsqrt(var + eps) * g + b

        def _selective_scan(x, delta, A, B_mat, C_mat, D_vec):
            dA = jnp.exp(delta[..., None] * A)
            Bx = jnp.einsum('bld,nd->bln', x, B_mat) * delta[..., None]

            def step(h, inp):
                dA_t, Bx_t = inp
                h = dA_t * h + Bx_t
                return (h, h)
            h0 = jnp.zeros((x.shape[0], A.shape[0]), x.dtype)
            _, hs = jax.lax.scan(step, h0, (jnp.swapaxes(dA, 0, 1), jnp.swapaxes(Bx, 0, 1)))
            hs = jnp.swapaxes(hs, 0, 1)
            return jnp.einsum('bln,dn->bld', hs, C_mat) + D_vec * x
        residual = x
        h = _layernorm(x, ln_gamma, ln_beta)
        xg = h @ W_in
        xs, gate = jnp.split(xg, 2, axis=-1)
        xc = jnp.swapaxes(xs, 1, 2)
        xc = jax.lax.conv_general_dilated(xc, conv_w, window_strides=(1,), padding=((K - 1, 0),), dimension_numbers=('NCH', 'OIH', 'NCH'), feature_group_count=D_INNER)
        xc = xc + conv_b[None, :, None]
        xs = jnp.swapaxes(xc, 1, 2)
        xs = jax.nn.silu(xs)
        delta = jnp.mean(jax.nn.softplus(xs @ Wd + bd), axis=-1)
        A = -jnp.exp(A_log)
        y = _selective_scan(xs, delta, A, B_mat, C_mat, D_vec)
        y = y * jax.nn.silu(gate)
        y = y @ W_out
        return residual + y

    def _L1_ffn_ref(x, Wq, keys, W_in, W_out, in_a, in_b, out_a, out_b):
        import jax, jax.numpy as jnp
        import numpy as np
        from jax import lax
        B, N, DIM = (4, 512, 256)
        HEADS = 8
        NUM_EXPERTS = 4096
        NUM_KEYS = 128
        DIM_KEY = DIM // 2
        DIM_INNER = 2 * DIM
        PK_TOPK = 16
        TOPK = 1
        b, n, d = x.shape
        q = (x @ Wq.T).reshape(b, n, 2, HEADS, DIM_KEY).transpose(2, 0, 1, 3, 4)
        sim = jnp.einsum('pbnhd,hkpd->pbnhk', q, keys)
        sx, ix = lax.top_k(sim[0], PK_TOPK)
        sy, iy = lax.top_k(sim[1], PK_TOPK)
        all_scores = (sx[..., :, None] + sy[..., None, :]).reshape(b, n, HEADS, PK_TOPK * PK_TOPK)
        all_indices = (ix[..., :, None] * NUM_KEYS + iy[..., None, :]).reshape(b, n, HEADS, PK_TOPK * PK_TOPK)
        scores, pk = lax.top_k(all_scores, TOPK)
        indices = jnp.take_along_axis(all_indices, pk, axis=-1)
        A_in = in_a[indices]
        B_in = in_b[indices]
        A_out = out_a[indices]
        B_out = out_b[indices]
        gate = jax.nn.relu(scores)
        hidden = x @ W_in.T
        lin = jnp.einsum('bnd,bnhkd->bnhk', x, A_in) * gate
        hidden = hidden + jnp.einsum('bnhk,bnhkd->bnd', lin, B_in)
        hidden = jax.nn.gelu(hidden, approximate=False)
        out = hidden @ W_out.T
        lout = jnp.einsum('bnd,bnhkd->bnhk', hidden, A_out) * gate
        out = out + jnp.einsum('bnhk,bnhkd->bnd', lout, B_out)
        return out

    def _L2_attn_ref(x, W_ret, b_ret, ln1_scale, ln1_bias, W1, b1, W2, b2, ln2_scale, ln2_bias):
        import jax, jax.numpy as jnp
        import numpy as np
        H = 256
        F = 1024
        B, S = (4, 1024)
        EPS = 1e-05

        def _layernorm(x, scale, bias):
            mu = jnp.mean(x, axis=-1, keepdims=True)
            var = jnp.var(x, axis=-1, keepdims=True)
            return (x - mu) * jax.lax.rsqrt(var + EPS) * scale + bias
        sig = jax.nn.sigmoid(jnp.einsum('bsh,hk->bsk', x, W_ret) + b_ret)

        def ema_step(carry, s_t):
            xi = 0.5 * s_t + 0.5 * carry
            return (xi, xi)
        _, ret = jax.lax.scan(ema_step, jnp.zeros((x.shape[0], x.shape[2]), x.dtype), jnp.transpose(sig, (1, 0, 2)))
        retention_output = jnp.transpose(ret, (1, 0, 2))
        h = _layernorm(x + retention_output, ln1_scale, ln1_bias)
        ffn = jnp.einsum('bsf,fh->bsh', jax.nn.gelu(jnp.einsum('bsh,hf->bsf', h, W1) + b1), W2) + b2
        out = _layernorm(h + ffn, ln2_scale, ln2_bias)
        return out

    def _L2_ffn_ref(x, k0, k1, k2, s0, s1, s2):
        import jax, jax.numpy as jnp
        import numpy as np
        import math
        D_IN = 256
        FEATURES = (1024, 1024, 256)
        BATCH, SEQ = (8, 512)

        def _conn_dense(kernel_bool, x):
            w = jnp.where(kernel_bool, jnp.float32(1.0), jnp.float32(-1.0))
            return x @ w
        h = jnp.concatenate([x, -x], axis=-1)
        h = s0 * _conn_dense(k0, h)
        h = jax.nn.relu(h) * 2
        h = s1 * _conn_dense(k1, h)
        h = jax.nn.relu(h) * 2
        h = s2 * _conn_dense(k2, h)
        return h

    def _L3_attn_ref(x, q_proj_weight, k_proj_weight, v_proj_weight, o_proj_weight):
        import jax, jax.numpy as jnp
        import numpy as np
        num_heads = 16
        B, S, d_in = x.shape
        d_k = q_proj_weight.shape[0]
        head_size = d_k // num_heads

        def split_heads(t):
            return t.reshape(B, S, num_heads, head_size).transpose(0, 2, 1, 3)
        q = split_heads(jnp.einsum('bsd,kd->bsk', x, q_proj_weight))
        k = split_heads(jnp.einsum('bsd,kd->bsk', x, k_proj_weight))
        v = split_heads(jnp.einsum('bsd,kd->bsk', x, v_proj_weight))
        scale = jnp.float32(head_size) ** (-0.5)
        scores = jnp.einsum('bhtc,bhkc->bhtk', q, k) * scale
        causal = jnp.tril(jnp.ones((S, S), dtype=bool))
        scores = jnp.where(causal, scores, -jnp.inf)
        attn = jax.nn.softmax(scores, axis=-1)
        out = jnp.einsum('bhtk,bhkc->bhtc', attn, v)
        out = out.transpose(0, 2, 1, 3).reshape(B, S, d_k)
        return jnp.einsum('bsv,dv->bsd', out, o_proj_weight)

    def _L3_ffn_ref(x, theta, phi, theta_noise, phi_noise):
        import jax, jax.numpy as jnp
        import numpy as np
        INPUT_SIZE = 256
        OUTPUT_SIZE = 256
        real = jnp.einsum('bti,io->bto', x, jnp.cos(theta + theta_noise))
        imag = jnp.einsum('bti,io->bto', x, jnp.sin(phi + phi_noise))
        return jnp.sqrt(real * real + imag * imag)
    x = L0_attn_x
    xn = _layernorm(x, axis=-1)
    x = x + _L0_attn_ref(xn, L0_attn_Wq, L0_attn_Wk, L0_attn_Wv, L0_attn_Wg, L0_attn_Wgk1, L0_attn_Wgk2, L0_attn_bgk2, L0_attn_Wo, L0_attn_g_norm_weight) + _L0_ffn_ref(xn, L0_ffn_Wr, L0_ffn_W1, L0_ffn_W2, L0_ffn_W3)
    xn = _layernorm(x, axis=-1)
    x = x + _L1_attn_ref(xn, L1_attn_ln_gamma, L1_attn_ln_beta, L1_attn_W_in, L1_attn_conv_w, L1_attn_conv_b, L1_attn_A_log, L1_attn_B_mat, L1_attn_C_mat, L1_attn_D_vec, L1_attn_Wd, L1_attn_bd, L1_attn_W_out) + _L1_ffn_ref(xn, L1_ffn_Wq, L1_ffn_keys, L1_ffn_W_in, L1_ffn_W_out, L1_ffn_in_a, L1_ffn_in_b, L1_ffn_out_a, L1_ffn_out_b)
    xn = _layernorm(x, axis=-1)
    x = x + _L2_attn_ref(xn, L2_attn_W_ret, L2_attn_b_ret, L2_attn_ln1_scale, L2_attn_ln1_bias, L2_attn_W1, L2_attn_b1, L2_attn_W2, L2_attn_b2, L2_attn_ln2_scale, L2_attn_ln2_bias) + _L2_ffn_ref(xn, L2_ffn_k0, L2_ffn_k1, L2_ffn_k2, L2_ffn_s0, L2_ffn_s1, L2_ffn_s2)
    xn = _layernorm(x, axis=-1)
    x = x + _L3_attn_ref(xn, L3_attn_q_proj_weight, L3_attn_k_proj_weight, L3_attn_v_proj_weight, L3_attn_o_proj_weight) + _L3_ffn_ref(xn, L3_ffn_theta, L3_ffn_phi, L3_ffn_theta_noise, L3_ffn_phi_noise)
    return x

_drawn_inputs = setup_inputs


def setup_inputs(seed=0):
    import zlib

    import numpy as np

    out = dict(_drawn_inputs(seed))
    spreads = {'L0_attn_bgk2': (0.0, 0.1),
     'L0_attn_g_norm_weight': (1.0, 0.2),
     'L1_attn_ln_gamma': (1.0, 0.2),
     'L1_attn_ln_beta': (0.0, 0.1),
     'L1_attn_conv_b': (0.0, 0.1),
     'L1_attn_bd': (0.0, 0.1),
     'L2_attn_b_ret': (0.0, 0.1),
     'L2_attn_ln1_scale': (1.0, 0.2),
     'L2_attn_ln1_bias': (0.0, 0.1),
     'L2_attn_b1': (0.0, 0.1),
     'L2_attn_b2': (0.0, 0.1),
     'L2_attn_ln2_scale': (1.0, 0.2),
     'L2_attn_ln2_bias': (0.0, 0.1)}
    factors = {}
    for name, (base, spread) in spreads.items():
        noise = np.random.default_rng([zlib.crc32(name.encode()), seed]).standard_normal(out[name].shape)
        drawn = base * np.exp(spread * noise) if base else spread * noise
        out[name] = jnp.asarray(drawn.astype(out[name].dtype))
    for name, factor in factors.items():
        out[name] = (out[name] * factor).astype(out[name].dtype)
    return out
```

```python
from contextlib import ExitStack

import concourse.bass as bass
from concourse import mybir

ALU = mybir.AluOpType
ACT = mybir.ActivationFunctionType
F32 = mybir.dt.float32
F32R = mybir.dt.float32r
BF16 = mybir.dt.bfloat16
U32 = mybir.dt.uint32
I32 = mybir.dt.int32
U8 = mybir.dt.uint8
AX = mybir.AxisListType

FIRST = 1
LAYERS = 4
T = 4096
NB = 8
BW = 512
SEQ = 2048
NEG = -1.0e30
EPS = 1e-5


class Queue:

    def __init__(self, sem):
        self.sem = sem
        self.n = 0
        self.items = []
        self.seen = {}

    def wait(self, *toks):
        for t in toks:
            if t is None:
                continue
            if isinstance(t, list):
                self.wait(*t)
                continue
            sem, val = t
            if self.seen.get(id(sem), 0) < val:
                self.seen[id(sem)] = val
                self.items.append((None, sem, val))

    def do(self, after, fn, *args, **kw):
        self.wait(*after)
        self.n += 1
        self.items.append((fn, args, kw, self.sem, 1))
        return (self.sem, self.n)

    def quiet(self, fn, *args, **kw):
        self.items.append((fn, args, kw, None, 0))

    def dma(self, after, sem, fn, *args, **kw):
        self.wait(*after)
        self.items.append((fn, args, kw, sem[0], 16))
        sem[1] += 16
        return (sem[0], sem[1])

    def last(self):
        return (self.sem, self.n) if self.n else None

    def emit(self, eng):
        for it in self.items:
            if it[0] is None:
                eng.wait_ge(it[1], it[2])
            else:
                ins = it[0](*it[1], **it[2])
                if it[3] is not None:
                    ins.then_inc(it[3], it[4])


class Slot:
    def __init__(self, ring, i):
        self.ring, self.i = ring, i
        self.ap = ring.bufs[i]
        self.free = ring.free[i]

    def release(self, *toks):
        assert self.ring.held[self.i]
        self.ring.held[self.i] = False
        self.ring.free[self.i] = list(toks)


class Ring:

    def __init__(self, bufs):
        self.bufs = bufs
        self.free = [[] for _ in bufs]
        self.held = [False for _ in bufs]
        self.i = 0

    def take(self):
        n = len(self.bufs)
        i = next(((self.i + j) % n for j in range(n) if not self.held[(self.i + j) % n]), self.i % n)
        self.i = i + 1
        assert not self.held[i], "slot taken before its readers are queued"
        self.held[i] = True
        return Slot(self, i)


def interleave(*gens):
    live = [[g, w, 0.0] for g, w in gens]
    while live:
        live.sort(key=lambda e: e[2])
        e = live[0]
        try:
            next(e[0])
            e[2] += e[1]
        except StopIteration:
            live.remove(e)


def build(nc, d, out):
    ctx = ExitStack()
    with ctx:
        def sem(name):
            return ctx.enter_context(nc.semaphore(name))

        PE, V, A, G, SP = (Queue(sem(n)) for n in ("s_pe", "s_dve", "s_act", "s_pool", "s_sp"))
        nvt, nvs = nc.vector.tensor_tensor, nc.vector.tensor_scalar
        stt = nc.vector.scalar_tensor_tensor
        act = nc.scalar.activation
        mmul = nc.tensor.matmul
        dsem = {}

        def dma(after, name, dst, src, q=None):
            if name not in dsem:
                dsem[name] = [sem(name), 0]
            q = q or SP
            return q.dma(after, dsem[name], nc.sync.dma_start, dst, src)

        def alloc(stack):
            def sb(name, shape, dt=F32):
                return stack.enter_context(nc.sbuf_tensor(name, shape, dt))
            return sb

        def group(after, mms):
            PE.wait(*after)
            for m in mms[:-1]:
                PE.quiet(mmul, m[0], m[1], m[2], start=m[3], stop=m[4], skip_group_check=True)
            m = mms[-1]
            return PE.do([], mmul, m[0], m[1], m[2], start=m[3], stop=m[4], skip_group_check=True)

        def transposes(after, pairs, ident):
            PE.wait(*after)
            for o, i in pairs[:-1]:
                PE.quiet(nc.tensor.transpose, o, i, ident)
            return PE.do([], nc.tensor.transpose, pairs[-1][0], pairs[-1][1], ident)

        def chain(o, ks):
            n = len(ks)
            return [(o, l, r, i == 0, i == n - 1) for i, (l, r) in enumerate(ks)]

        def barrier():
            toks = [q.last() for q in (PE, V, A, G)] + [(s[0], s[1]) for s in dsem.values() if s[1]]
            for q in (PE, V, A, G, SP):
                q.wait(*toks)

        sb = alloc(ctx)
        PS = [ctx.enter_context(nc.psum_tensor(f"ps{i}", [128, 512], F32)) for i in range(8)]
        xT = sb("xT", [128, 2, T])
        xn = sb("xn", [128, 2, T])
        ident = sb("ident", [128, 128])
        identb = sb("identb", [128, 128], BF16)
        onesm = sb("onesm", [128, 128])
        epsc = sb("epsc", [128, 1])
        onec = sb("onec", [128, 1])

        xload = [dma([], f"x{n}", xT[:, :, n * BW:(n + 1) * BW], d["x"][:, :, n * BW:(n + 1) * BW])
                 for n in range(NB)]

        g1 = G.do([], nc.gpsimd.memset, ident[:, :], 0.0)
        g1 = G.do([g1], nc.gpsimd.affine_select, out=ident[:, :], in_=ident[:, :], compare_op=ALU.not_equal,
                  fill=1.0, base=0, pattern=[[-1, 128]], channel_multiplier=1)
        c_idb = V.do([g1], nc.vector.tensor_copy, identb[:, :], ident[:, :])
        V.do([], nc.vector.memset, onesm[:, :], 1.0 / 256.0)
        V.do([], nc.vector.memset, epsc[:, :], EPS)
        c_one = V.do([], nc.vector.memset, onec[:, :], 1.0)

        xw = {n: None for n in range(NB)}

        def blk(t, k, n):
            return t[:, k, n * BW:(n + 1) * BW]

        def norm_stages(src, src_ready, dst, R, ring_t, psr, scale_bias=None, dst_free=(),
                        mul=G):
            p = psr.take()
            t1 = group([src_ready, p.free, c_one], chain(p.ap[:, :], [(onesm[:, :], src[:, k, :]) for k in range(2)]))
            xc = ring_t.take()
            v1 = V.do([t1, xc.free], nvt, xc.ap[:, :, :], src, p.ap[:, None, :].broadcast_to([128, 2, BW]),
                      ALU.subtract)
            p.release(v1)
            sq = ring_t.take()
            a1 = A.do([v1, sq.free], act, sq.ap[:, :, :], xc.ap[:, :, :], ACT.Square)
            yield
            p = psr.take()
            t2 = group([a1, p.free], chain(p.ap[:, :], [(onesm[:, :], sq.ap[:, k, :]) for k in range(2)]))
            a2 = A.do([t2], act, sq.ap[:, 0, :], p.ap[:, :], ACT.Sqrt, bias=epsc[:, 0:1])
            p.release(a2)
            v2 = V.do([a2], nc.vector.reciprocal, sq.ap[:, 1, :], sq.ap[:, 0, :])
            rb = sq.ap[:, 1:2, :].broadcast_to([128, 2, BW])
            if scale_bias is None:
                tok = (G.do([v2, *dst_free], nc.gpsimd.tensor_tensor, dst, xc.ap[:, :, :], rb, ALU.mult)
                       if mul is G else V.do([v2, *dst_free], nvt, dst, xc.ap[:, :, :], rb, ALU.mult))
                xc.release(tok)
                sq.release(tok)
            else:
                s_, b_ = scale_bias
                own = dst is None
                dst = xc.ap if own else dst
                g_ = (G.do([v2], nc.gpsimd.tensor_tensor, xc.ap[:, :, :], xc.ap[:, :, :], rb, ALU.mult)
                      if mul is G else V.do([v2], nvt, xc.ap[:, :, :], xc.ap[:, :, :], rb, ALU.mult))
                sq.release(g_)
                for k in range(2):
                    tok = V.do([g_, *dst_free], nvs, dst[:, k, :], xc.ap[:, k, :], s_[:, k:k + 1], b_[:, k:k + 1],
                               ALU.mult, ALU.add)
                if own:
                    R.append(xc)
                else:
                    xc.release(tok)
            R.append(tok)

        def layer_norm_all(src_ready, ring_t, psr):
            toks = [[] for _ in range(NB)]
            gens = [norm_stages(xT[:, :, n * BW:(n + 1) * BW], src_ready[n], xn[:, :, n * BW:(n + 1) * BW],
                                toks[n], ring_t, psr) for n in range(NB)]
            for n in range(NB + 1):
                if n < NB:
                    next(gens[n])
                if n > 0:
                    for _ in gens[n - 1]:
                        pass
            return [t[0] for t in toks]

        def xs(n, k):
            return blk(xn, k, n)

        def layer0(ready):
            ph = ExitStack()
            sb = alloc(ph)
            Wq, Wk = sb("Wq", [128, 2, 256]), sb("Wk", [128, 2, 256])
            Wv, Wg = sb("Wv", [128, 2, 512]), sb("Wg", [128, 2, 512])
            W1g = sb("Wgk1", [128, 2, 16])
            low = sb("low", [64, BW + 256])
            W2g = low[32:48, BW:BW + 256]
            g16 = low[32:48, 0:BW]
            combT = low[0:8, 0:BW]
            Wo = sb("Wo", [128, 4, 256])
            vec = sb("vec0", [128, 3])
            Wr = sb("Wr", [128, 2, 8])
            F1, F3 = sb("F1", [128, 8, 2, 384]), sb("F3", [128, 8, 2, 384])
            F2 = sb("F2", [128, 8, 3, 256])
            for t_, n_ in ((Wr, "Wr"), (W1g, "Wgk1"), (Wq, "Wq"), (Wk, "Wk"), (Wv, "Wv"), (Wg, "Wg"), (Wo, "Wo")):
                w_att = dma([], "w0", t_[:, :, :], d[n_])
            w_att = dma([], "w0", W2g, d["Wgk2"])
            w_att = dma([], "w0", vec[:, :], d["vec0"])
            w_ffn = []
            for e in range(8):
                for t_, n_ in ((F1, "F1"), (F3, "F3"), (F2, "F2")):
                    tok = dma([], f"w0f{e}", t_[:, e, :, :], d[n_][:, e, :, :])
                w_ffn.append(tok)
            psa = Ring(PS[0:3])
            psf = Ring(PS[3:6])
            pacc = Ring(PS[6:8])
            QK = sb("QK", [128, 4, BW])
            ob = sb("ob", [128, 4, BW])
            lnr = layer_norm_all(ready, Ring([t_[:, i:i + 2, :] for t_ in (QK, ob) for i in (0, 2)]), psf)
            hw = Ring([sb(f"hw{i}", [128, BW]) for i in range(4)])

            tri01 = sb("tri01", [128, 1, 128])
            g2 = G.do([], nc.gpsimd.memset, tri01[:, :, :], 1.0)
            c_tri = G.do([g2], nc.gpsimd.affine_select, out=tri01[:, :, :], in_=tri01[:, :, :],
                         compare_op=ALU.is_ge, fill=0.0, base=0, pattern=[[0, 1], [1, 128]], channel_multiplier=-1)
            resm = sb("resm", [128, 4, 128])
            c_res = G.do([], nc.gpsimd.memset, resm[:, :, :], 1.0)
            c_res = G.do([c_res], nc.gpsimd.memset, resm[:, :, 0:1], 0.0)
            ones128 = sb("ones128", [128, 128])
            c_o128 = V.do([], nc.vector.memset, ones128[:, :], 1.0 / 128.0)
            S = sb("S", [128, 2, 128])
            Ss = sb("Ss", [128, 4, 128])
            z_ss = V.do([], nc.vector.memset, Ss[:, :, :], 0.0)
            U2 = sb("U2", [128, 2, 128])
            cum = sb("cum", [128, BW])
            D = sb("D", [128, BW])
            ex = Ring([sb(f"ex{i}", [128, BW]) for i in range(2)])
            qh, kh = [QK[:, i, :] for i in range(2)], [QK[:, 2 + i, :] for i in range(2)]
            ebm, ebe, eem = (sb(n_, [128, 2, 4]) for n_ in ("ebm", "ebe", "eem"))
            vr = Ring([sb(f"vt{i}", [128, 512]) for i in range(2)])
            at = sb("at", [128, 4, 128])
            kt = sb("kt", [128, 256])
            st = {"ob": [lnr[-1]], "qk": [lnr[-1]], "e": [], "S": None, "Ss": None, "g16": None,
                  "at": None, "kt": None, "U2": None, "cum": None, "D": None}
            done = []

            def attn():
                for n in range(NB):
                    lr = lnr[n]
                    p = psa.take()
                    t_ = group([lr, w_att, p.free], chain(p.ap[0:16, :], [(W1g[:, k, :], xs(n, k)) for k in range(2)]))
                    v_ = V.do([t_, st["g16"]], nc.vector.tensor_copy, g16, p.ap[0:16, :])
                    p.release(v_)
                    for j in range(2):
                        yield
                        p = psa.take()
                        t_ = group([v_, p.free], [(p.ap[:, :], W2g[:, j * 128:(j + 1) * 128], g16, True, True)])
                        st["g16"] = t_
                        e1, e2 = ex.take(), ex.take()
                        a_ = A.do([t_, e1.free], act, e1.ap[:, :], p.ap[:, :], ACT.Abs, bias=vec[:, j:j + 1])
                        a_ = A.do([a_], act, e1.ap[:, :], e1.ap[:, :], ACT.Exp, scale=-1.0)
                        a_ = A.do([a_, c_one], act, e1.ap[:, :], e1.ap[:, :], ACT.Ln, bias=onec[:, 0:1])
                        m_ = V.do([t_, a_, e2.free], nvs, e2.ap[:, :], p.ap[:, :], vec[:, j:j + 1], 0.0, ALU.add,
                                  ALU.min)
                        p.release(m_)
                        m_ = V.do([m_, a_], nvt, e2.ap[:, :], e2.ap[:, :], e1.ap[:, :], ALU.subtract)
                        e1.release(m_)
                        c_ = V.do([m_, c_res, st["cum"]], nc.vector.tensor_tensor_scan, cum[:, :],
                                  resm[:, :, :].rearrange("p a b -> p (a b)"), e2.ap[:, :], 0.0, ALU.mult, ALU.add)
                        e2.release(c_)
                        cv = cum[:, :].rearrange("p (c t) -> p c t", c=4)
                        dv = D[:, :].rearrange("p (c t) -> p c t", c=4)
                        d_ = V.do([c_, st["D"]], nvt, dv, cv, cv[:, :, 63:64].broadcast_to([128, 4, 128]),
                                  ALU.subtract)
                        a1 = A.do([d_, *st["e"]], act, ebm[:, j, :], cv[:, :, 63], ACT.Exp, scale=1 / 16)
                        a1 = A.do([], act, ebe[:, j, :], cv[:, :, 127], ACT.Exp, scale=1 / 16)
                        a1 = A.do([], act, eem[:, j, :], dv[:, :, 127], ACT.Exp, scale=1 / 16)
                        st["cum"] = a1
                        e1, e2 = ex.take(), ex.take()
                        aq = A.do([d_, e1.free], act, e1.ap[:, :], D[:, :], ACT.Exp, scale=1 / 16)
                        ak = A.do([e2.free], act, e2.ap[:, :], D[:, :], ACT.Exp, scale=-1 / 16)
                        st["D"] = ak
                        yield
                        for w_, o_, e_, sc_, a_ in ((Wq, qh, e1, 0.125, aq), (Wk, kh, e2, 1.0, ak)):
                            p = psa.take()
                            t_ = group([p.free], chain(p.ap[:, :], [(w_[:, k, j * 128:(j + 1) * 128], xs(n, k))
                                                                    for k in range(2)]))
                            s_ = V.do([t_, a_, *st["qk"]], stt, out=o_[j], in0=p.ap[:, :], scalar=sc_,
                                      in1=e_.ap[:, :], op0=ALU.mult, op1=ALU.mult)
                            e_.release(s_)
                            p.release(s_)
                    qk_ready = s_
                    e_ready = a1
                    if n % 4 == 0:
                        st["S"] = V.do([st["S"], st["Ss"]], nc.vector.memset, S[:, :, :], 0.0)
                    for c in range(4):
                        cs = slice(c * 128, (c + 1) * 128)
                        yield
                        p = psa.take()
                        t_ = group([p.free], chain(p.ap[:, :], [
                            (xn[:, k, n * BW + c * 128:n * BW + (c + 1) * 128], Wv[:, k, :]) for k in range(2)]))
                        vs = vr.take()
                        vt = vs.ap
                        vtk = A.do([t_, vs.free], act, vt[:, :], p.ap[:, :], ACT.Copy)
                        p.release(vtk)
                        for h in range(4):
                            hs = slice(64 * (h % 2), 64 * (h % 2) + 64)
                            ss = V.do([st["S"], st["Ss"], e_ready, z_ss], nvs, Ss[hs, h, :], S[hs, h // 2, :],
                                      ebm[hs, h // 2, c:c + 1], None, ALU.mult)
                        yield
                        p = psa.take()
                        t_ = transposes([qk_ready, g1, p.free], [(p.ap[:, j * 128:(j + 1) * 128], kh[j][:, cs])
                                                                  for j in range(2)], ident[:, :])
                        ktk = V.do([t_, st["kt"]], nc.vector.tensor_copy, kt[:, :], p.ap[:, 0:256])
                        p.release(ktk)
                        pp = [psa.take(), psa.take()]
                        mms = []
                        for h in (0, 2, 1, 3):
                            hs = slice(64 * (h % 2), 64 * (h % 2) + 64)
                            mms.append((pp[h % 2].ap[:, (h // 2) * 128:(h // 2 + 1) * 128], kh[h // 2][hs, cs],
                                        qh[h // 2][hs, cs], True, True))
                        t_ = group([pp[0].free, pp[1].free], mms)
                        for hh in range(2):
                            att = V.do([t_, c_tri, st["at"]], nvt, at[:, hh:4:2, :],
                                       pp[hh].ap[:, 0:256].rearrange("p (h t) -> p h t", h=2),
                                       tri01[:, :, :].broadcast_to([128, 2, 128]), ALU.mult)
                            pp[hh].release(att)
                        yield
                        p = psa.take()
                        mms = []
                        for h in range(4):
                            o_ = p.ap[:, h * 128:(h + 1) * 128]
                            mms.append((o_, vt[:, h * 128:(h + 1) * 128], at[:, h, :], True, False))
                            mms.append((o_, Ss[:, h, :], qh[h // 2][:, cs], False, True))
                        to = group([att, ss, vtk, p.free], mms)
                        st["at"] = st["Ss"] = to
                        obt = A.do([to, *st["ob"]], act, ob[:, :, cs],
                                   p.ap[:, :].rearrange("p (h t) -> p h t", h=4), ACT.Copy)
                        p.release(obt)
                        p = psa.take()
                        tu = group([ktk, p.free], [(p.ap[:, j * 256:(j + 1) * 256], kt[:, j * 128:(j + 1) * 128],
                                                    vt[:, j * 256:(j + 1) * 256], True, True) for j in range(2)])
                        st["kt"] = tu
                        vs.release(tu)
                        for j in range(2):
                            for h in range(2):
                                hs = slice(64 * h, 64 * h + 64)
                                u_ = V.do([tu, st["U2"], e_ready], nvs, U2[hs, j, :],
                                          p.ap[hs, j * 256 + h * 128:j * 256 + (h + 1) * 128], eem[hs, j, c:c + 1],
                                          None, ALU.mult)
                        p.release(u_)
                        for j in range(2):
                            s_ = V.do([u_, ss], stt, out=S[:, j, :], in0=S[:, j, :], scalar=ebe[:, j, c:c + 1],
                                      in1=U2[:, j, :], op0=ALU.mult, op1=ALU.add)
                        st["U2"] = st["S"] = s_
                    st["qk"], st["e"] = [tu, to], [s_]
                    yield
                    pr = []
                    for h in range(4):
                        e1 = ex.take()
                        a_ = A.do([obt, e1.free], act, e1.ap[:, :], ob[:, h, :], ACT.Square)
                        p = psa.take()
                        t_ = group([a_, c_o128, p.free], [(p.ap[:, :], ones128[:, :], e1.ap[:, :], True, True)])
                        a_ = A.do([t_], act, e1.ap[:, :], p.ap[:, :], ACT.Sqrt, bias=epsc[:, 0:1])
                        p.release(a_)
                        v_ = V.do([a_], nc.vector.reciprocal, e1.ap[:, :], e1.ap[:, :])
                        v_ = V.do([v_], stt, out=ob[:, h, :], in0=ob[:, h, :], scalar=vec[:, 2:3],
                                  in1=e1.ap[:, :], op0=ALU.mult, op1=ALU.mult)
                        e1.release(v_)
                        p = psa.take()
                        t_ = group([p.free], chain(p.ap[:, :], [(Wg[:, k, h * 128:(h + 1) * 128], xs(n, k))
                                                                for k in range(2)]))
                        e1 = ex.take()
                        a_ = A.do([t_, e1.free], act, e1.ap[:, :], p.ap[:, :], ACT.Silu)
                        p.release(a_)
                        pr.append(G.do([v_, a_], nc.gpsimd.tensor_tensor, ob[:, h, :], ob[:, h, :], e1.ap[:, :],
                                       ALU.mult))
                        e1.release(pr[-1])
                        yield
                    for m in range(2):
                        p = psa.take()
                        t_ = group([pr[-1], p.free], chain(p.ap[:, :], [(Wo[:, h, m * 128:(m + 1) * 128], ob[:, h, :])
                                                                        for h in range(4)]))
                        v_ = xw[n] = V.do([t_, xw[n]], nvt, blk(xT, m, n), blk(xT, m, n), p.ap[:, :], ALU.add)
                        p.release(v_)
                    st["ob"] = [t_]
                    done.append(v_)
                    yield

            iot = sb("iot", [128, 8])
            ioti = sb("ioti", [128, 8], I32)
            c_io = G.do([], nc.gpsimd.iota, ioti[:, :], pattern=[[1, 8]], base=0, channel_multiplier=0)
            c_io = V.do([c_io], nc.vector.tensor_copy, iot[:, :], ioti[:, :])
            lg = sb("lg", [128, 4, 8])
            m8 = sb("m8", [128, 4, 8])
            ix = sb("ix", [128, 4, 8], U32)
            ixf = sb("ixf", [128, 4, 8])
            w8 = sb("w8", [128, 4, 4])
            cb1 = sb("cb1", [128, 4, 8])
            cb2 = sb("cb2", [128, 4, 8])
            cbs = Ring([sb(f"cbs{i}", [128, BW]) for i in range(2)])
            cfree = []
            fdone = []

            def gate_weights(n):
                p = psf.take()
                mms = []
                for c in range(4):
                    mms += chain(p.ap[:, c * 8:(c + 1) * 8], [
                        (xn[:, k, n * BW + c * 128:n * BW + (c + 1) * 128], Wr[:, k, :]) for k in range(2)])
                t_ = group([lnr[n], w_att, p.free], mms)
                v_ = V.do([t_, V.last()], nc.vector.tensor_copy, lg[:, :, :].rearrange("p a b -> p (a b)"),
                          p.ap[:, 0:32])
                p.release(v_)
                for c in range(4):
                    v1 = V.do([v_], nc.vector.max, m8[:, c, :], lg[:, c, :])
                for c in range(4):
                    v2 = V.do([v1], nc.vector.max_index, ix[:, c, :], m8[:, c, :], lg[:, c, :])
                v2 = V.do([v2], nc.vector.tensor_copy, ixf[:, :, :], ix[:, :, :])
                v3 = V.do([v1], nvt, w8[:, :, 0:1], m8[:, :, 1:2], m8[:, :, 0:1], ALU.subtract)
                a_ = A.do([v3], act, w8[:, :, 1:2], w8[:, :, 0:1], ACT.Exp)
                v3 = V.do([a_], nvs, w8[:, :, 2:3], w8[:, :, 1:2], 1.0, None, ALU.add)
                v3 = V.do([v3], nc.vector.reciprocal, w8[:, :, 2:3], w8[:, :, 2:3])
                v3 = V.do([v3, v2], nvt, w8[:, :, 3:4], w8[:, :, 1:2], w8[:, :, 2:3], ALU.mult)
                for c in range(4):
                    V.do([v3, c_io], nvs, cb1[:, c, :], iot[:, :], ixf[:, c, 0:1], w8[:, c, 2:3], ALU.is_equal,
                         ALU.mult)
                    v4 = V.do([v3, c_io], nvs, cb2[:, c, :], iot[:, :], ixf[:, c, 1:2], w8[:, c, 3:4],
                              ALU.is_equal, ALU.mult)
                v4 = V.do([v4], nvt, cb1[:, :, :], cb1[:, :, :], cb2[:, :, :], ALU.add)
                yield
                p = psf.take()
                t_ = transposes([v4, g1, p.free], [(p.ap[0:8, c * 128:(c + 1) * 128], cb1[:, c, :])
                                                   for c in range(4)], ident[:, :])
                v_ = V.do([t_, *cfree], nc.vector.tensor_copy, combT, p.ap[0:8, :])
                p.release(v_)
                return v_

            def ffn():
                cr = yield from gate_weights(0)
                for n in range(NB):
                    acc = [pacc.take(), pacc.take()]
                    pend = None
                    for e in range(8):
                        p = psf.take()
                        t_ = group([cr, g1, p.free], [(p.ap[:, :], ident[0:8, e:e + 1].broadcast_to([8, 128]), combT,
                                                   True, True)])
                        cb = cbs.take()
                        cbt = A.do([t_, cb.free], act, cb.ap[:, :], p.ap[:, :], ACT.Copy)
                        p.release(cbt)
                        for m in range(3):
                            ms = slice(m * 128, (m + 1) * 128)
                            ph_, pg_ = psf.take(), psf.take()
                            th = group([w_ffn[e], ph_.free], chain(ph_.ap[:, :], [(F1[:, e, k, ms], xs(n, k))
                                                                                  for k in range(2)]))
                            s_ = hw.take()
                            a_ = A.do([th, s_.free], act, s_.ap[:, :], ph_.ap[:, :], ACT.Silu)
                            ph_.release(a_)
                            tg = group([pg_.free], chain(pg_.ap[:, :], [(F3[:, e, k, ms], xs(n, k))
                                                                        for k in range(2)]))
                            v_ = V.do([tg, a_], nvt, s_.ap[:, :], s_.ap[:, :], pg_.ap[:, :], ALU.mult)
                            pg_.release(v_)
                            g_ = G.do([v_, cbt], nc.gpsimd.tensor_tensor, s_.ap[:, :], s_.ap[:, :], cb.ap[:, :],
                                      ALU.mult)
                            if m == 2:
                                cb.release(g_)
                            yield
                            if pend is not None:
                                down(acc, *pend)
                            pend = (s_, g_, e, m)
                    cfree[:] = [t_]
                    if n + 1 < NB:
                        cr = yield from gate_weights(n + 1)
                    ta = down(acc, *pend)
                    for m in range(2):
                        v_ = xw[n] = V.do([ta, xw[n]], nvt, blk(xT, m, n), blk(xT, m, n), acc[m].ap[:, :], ALU.add)
                        acc[m].release(v_)
                    fdone.append(v_)

            def down(acc, s_, g_, e, m):
                mms = [(acc[o].ap[:, :], F2[:, e, m, o * 128:(o + 1) * 128], s_.ap[:, :], e == 0 and m == 0,
                        e == 7 and m == 2) for o in range(2)]
                ta = group([g_] + (acc[0].free + acc[1].free if e == 0 and m == 0 else []), mms)
                s_.release(ta)
                return ta

            interleave((attn(), 1.6), (ffn(), 1.0))
            barrier()
            ph.close()
            return [[done[n], fdone[n]] for n in range(NB)]

        def layer1(ready):
            ph = ExitStack()
            sb = alloc(ph)
            GA, GB = sb("gathA", [128, 8, 768]), sb("gathB", [128, 8, 768])
            Wi = sb("mWi", [128, 2, 1024])
            Wd = sb("mWd", [128, 4, 512])
            Wu = sb("mWo", [128, 4, 256])
            Bm = sb("mB", [128, 4, 16])
            Cm = sb("mC", [16, 512])
            Al = sb("mA", [16, 1])
            vec = sb("vec1", [128, 32])
            cw = sb("mcw", [128, 4, 4])
            Pi = sb("pWi", [128, 2, 512])
            Po = sb("pWo", [128, 4, 256])
            WS = sb("WS", [128, 2, 2048])
            gflat = GA[:, :, :].rearrange("p a b -> p (a b)")
            WqK = gflat[:, 0:4096].rearrange("p (a b) -> p a b", a=16)
            keys = gflat[:, 4096:6144].rearrange("p (a b) -> p a b", a=16)
            w_k = dma([], "w1k", WqK, d["pWq"])
            w_k = dma([], "w1k", keys, d["keys"])
            for t_, n_ in ((Wi, "mWi"), (Wd, "mWd"), (Wu, "mWo"), (Bm, "mB"), (cw, "mcw")):
                w_m = dma([], "w1m", t_[:, :, :], d[n_])
            for t_, n_ in ((Cm, "mC"), (Al, "mA"), (vec, "vec1")):
                w_m = dma([], "w1m", t_[:, :], d[n_])
            for t_, n_ in ((Pi, "pWi"), (Po, "pWo")):
                w_p = dma([], "w1p", t_[:, :, :], d[n_])
            gam, bet, cvb, bd, Dv = vec[:, 0:2], vec[:, 2:4], vec[:, 4:8], vec[:, 8:12], vec[:, 12:16]
            psm = Ring(PS[0:3])
            psk = Ring(PS[3:8])
            xsb = sb("xsb", [128, 4, 3 + BW])
            u = sb("u", [128, 4, BW])
            big = Ring([sb(f"bg{i}", [128, 2, BW]) for i in range(2)])
            lnr = layer_norm_all(ready, Ring([b_ for b_ in big.bufs] + [u[:, 0:2, :], u[:, 2:4, :]]), psm)
            big.free = [[lnr[-1]], [lnr[-1]]]
            wst = []
            for kk in range(2):
                for g in range(4):
                    p = psk.take()
                    t_ = group([w_k, p.free], [(p.ap[:, i * 128:(i + 1) * 128],
                                                WqK[:, 4 * g + i, kk * 128:(kk + 1) * 128], keys[:, 4 * g + i, :],
                                                True, True) for i in range(4)])
                    wst.append(A.do([t_], act, WS[:, kk, g * 512:(g + 1) * 512], p.ap[:, :], ACT.Copy))
                    p.release(wst[-1])
            ws_used = t_
            sA = sb("sA", [16, 1])
            a_ = A.do([w_m], act, sA[:, :], Al[:, :], ACT.Exp)
            c_A = A.do([a_], act, sA[:, :], sA[:, :], ACT.Copy, scale=-1.0)
            o16 = sb("o16", [128, 16])
            c_o16 = V.do([], nc.vector.memset, o16[:, :], 1.0 / 512.0)
            tmp = Ring([sb(f"tm{i}", [128, BW]) for i in range(4)])
            dl = sb("dl", [16, BW])
            Bx = hs = sb("Bx", [16, BW])
            done, fdone = [], []

            def mamba():
                s = {"xsb": [], "u": [lnr[-1]], "dl": [], "Bx": [], "halo": None}
                for n in range(NB):
                    R = []
                    yield from norm_stages(xn[:, :, n * BW:(n + 1) * BW], lnr[n], None, R, big, psm,
                                           (gam, bet), dst_free=[w_m], mul=V)
                    hslot, hr = R
                    hn = hslot.ap
                    yield
                    if n % 4 == 0:
                        hal = V.do([*s["xsb"]], nc.vector.memset, xsb[:, :, 0:3], 0.0)
                    else:
                        hal = V.do([*s["xsb"]], nc.vector.tensor_copy, xsb[:, :, 0:3], xsb[:, :, BW:BW + 3])
                    ur = []
                    for i in range(4):
                        p = psm.take()
                        t_ = group([hr, p.free], chain(p.ap[:, :], [(Wi[:, k, i * 128:(i + 1) * 128], hn[:, k, :])
                                                                    for k in range(2)]))
                        a_ = A.do([t_, hal], act, xsb[:, i, 3:3 + BW], p.ap[:, :], ACT.Copy)
                        p.release(a_)
                        c1 = tmp.take()
                        v_ = V.do([a_, c1.free], nvs, c1.ap[:, :], xsb[:, i, 0:BW], cw[:, i, 0:1], None, ALU.mult)
                        for k in range(1, 4):
                            v_ = V.do([v_], stt, out=c1.ap[:, :], in0=xsb[:, i, k:k + BW], scalar=cw[:, i, k:k + 1],
                                      in1=c1.ap[:, :], op0=ALU.mult, op1=ALU.add)
                        ur.append(A.do([v_, *s["u"]], act, u[:, i, :], c1.ap[:, :], ACT.Silu, bias=cvb[:, i:i + 1]))
                        c1.release(ur[-1])
                        yield
                    s["xsb"] = [v_]
                    pb = psm.take()
                    tb = group([ur[3], pb.free], chain(pb.ap[0:16, :], [(Bm[:, k, :], u[:, k, :]) for k in range(4)]))
                    bxa = A.do([tb, *s["Bx"]], act, Bx[:, :], pb.ap[0:16, :], ACT.Copy)
                    pb.release(bxa)
                    sp = []
                    for i in range(4):
                        p = psm.take()
                        t_ = group([p.free], chain(p.ap[:, :], [(Wd[:, k, i * 128:(i + 1) * 128], u[:, k, :])
                                                                for k in range(4)]))
                        e1, e2 = tmp.take(), tmp.take()
                        rl = e2.ap[:, :]
                        a_ = A.do([t_, e1.free], act, e1.ap[:, :], p.ap[:, :], ACT.Abs, bias=bd[:, i:i + 1])
                        v_ = V.do([a_, e2.free], nvs, rl, p.ap[:, :], bd[:, i:i + 1], 0.0, ALU.add, ALU.max)
                        p.release(v_)
                        a_ = A.do([a_], act, e1.ap[:, :], e1.ap[:, :], ACT.Exp, scale=-1.0)
                        yield
                        if i == 0:
                            pd = psm.take()
                            pe1 = e1
                            pv_ = V.do([a_], nvs, e1.ap[:, :], e1.ap[:, :], 1.0, None, ALU.add)
                        else:
                            pv_ = V.do([a_, pv_], stt, out=pe1.ap[:, :], in0=e1.ap[:, :], scalar=1.0,
                                       in1=pe1.ap[:, :], op0=ALU.add, op1=ALU.mult)
                            e1.release(pv_)
                        td = group([v_, c_o16, pd.free], [(pd.ap[0:16, :], o16[:, :], rl, i == 0, False)])
                        e2.release(td)
                    a_ = A.do([pv_], act, pe1.ap[:, :], pe1.ap[:, :], ACT.Ln)
                    yield
                    td = group([a_], [(pd.ap[0:16, :], o16[:, :], pe1.ap[:, :], False, True)])
                    pe1.release(td)
                    v_ = V.do([td, *s["dl"]], nc.vector.tensor_copy, dl[:, :], pd.ap[0:16, :])
                    pd.release(v_)
                    v_ = V.do([v_, bxa], nvt, Bx[:, :], Bx[:, :], dl[:, :], ALU.mult)
                    a_ = A.do([v_, c_A], act, dl[:, :], dl[:, :], ACT.Exp, scale=sA[:, 0:1])
                    init = 0.0 if n % 4 == 0 else hl[:, 0:1]
                    v_ = V.do([v_, a_, s["halo"]], nc.vector.tensor_tensor_scan, hs[:, :], dl[:, :],
                              Bx[:, :], init, ALU.mult, ALU.add)
                    s["dl"] = [v_]
                    s["halo"] = V.do([v_], nc.vector.tensor_copy, hl[:, 0:1], hs[:, BW - 1:BW])
                    yield
                    for i in range(4):
                        p = psm.take()
                        t_ = group([v_, p.free], [(p.ap[:, :], Cm[:, i * 128:(i + 1) * 128], hs[:, :], True, True)])
                        y_ = V.do([t_, ur[i]], stt, out=u[:, i, :], in0=u[:, i, :], scalar=Dv[:, i:i + 1],
                                  in1=p.ap[:, :], op0=ALU.mult, op1=ALU.add)
                        p.release(y_)
                        p = psm.take()
                        t_ = group([p.free], chain(p.ap[:, :], [(Wi[:, k, 512 + i * 128:512 + (i + 1) * 128],
                                                                 hn[:, k, :]) for k in range(2)]))
                        e1 = tmp.take()
                        gt = A.do([t_, e1.free], act, e1.ap[:, :], p.ap[:, :], ACT.Silu)
                        p.release(gt)
                        y_ = V.do([y_, gt], nvt, u[:, i, :], u[:, i, :], e1.ap[:, :], ALU.mult)
                        e1.release(y_)
                        yield
                    s["Bx"] = [t_, s["halo"]]
                    hslot.release(t_)
                    for m in range(2):
                        p = psm.take()
                        t_ = group([y_, p.free], chain(p.ap[:, :], [(Wu[:, k, m * 128:(m + 1) * 128], u[:, k, :])
                                                                    for k in range(4)]))
                        v_ = xw[n] = V.do([t_, xw[n]], nvt, blk(xT, m, n), blk(xT, m, n), p.ap[:, :], ALU.add)
                        p.release(v_)
                        v_ = xw[n] = V.do([v_], nvt, blk(xT, m, n), blk(xT, m, n), blk(xn, m, n), ALU.add)
                    s["u"] = [t_]
                    done.append(v_)
                    yield

            hl = sb("hl", [16, 1])
            mx = sb("mx", [128, 16, 8])
            mi = sb("mi", [128, 16, 8], U32)
            mif = sb("mif", [128, 16])
            idx = Ring([sb(f"idx{i}", [128, 8], U32) for i in range(3)])
            gte = Ring([sb(f"gte{i}", [128, 8]) for i in range(3)])
            gf = sb("gf", [128, 16])
            xt_ = sb("xt_", [128, 256])
            lin = sb("lin", [128, 16])
            hacc = sb("hacc", [128, 512])
            hg = sb("hg", [128, 512])
            jk = sb("jk", [128, 512])
            oacc = sb("oacc", [128, 256])
            hgT = sb("hgT", [128, 512])
            NT = 32

            def route(t, q):
                ts = slice(t * 128, (t + 1) * 128)
                for g in range(4):
                    p = psk.take()
                    tk = group([lnr[t // 4], wst[g], wst[4 + g], p.free], chain(p.ap[:, :], [
                        (xn[:, k, ts], WS[:, k, g * 512:(g + 1) * 512]) for k in range(2)]))
                    for i in range(4):
                        v1 = V.do([tk, q["mx"]], nc.vector.max, mx[:, 4 * g + i, :], p.ap[:, i * 128:(i + 1) * 128])
                    for i in range(4):
                        v2 = V.do([v1], nc.vector.max_index, mi[:, 4 * g + i, :], mx[:, 4 * g + i, :],
                                  p.ap[:, i * 128:(i + 1) * 128])
                    p.release(v2)
                    yield
                v3 = V.do([v2, q["mif"]], nc.vector.tensor_copy, mif[:, :], mi[:, :, 0])
                v4 = V.do([v3], stt, out=gf[:, 0:8], in0=mif[:, 0:8], scalar=128.0, in1=mif[:, 8:16], op0=ALU.mult,
                          op1=ALU.add)
                id_, gt_ = idx.take(), gte.take()
                v5 = V.do([v4, id_.free], nvs, id_.ap[:, :], gf[:, 0:8], 4095.0, None, ALU.min)
                q["mif"] = v5
                v6 = V.do([v1, gt_.free], nvt, gt_.ap[:, :], mx[:, 0:8, 0], mx[:, 8:16, 0], ALU.add)
                v6 = V.do([v6], nvs, gt_.ap[:, :], gt_.ap[:, :], 0.0, None, ALU.max)
                q["mx"] = v6
                q["out"] = (id_, gt_, v5, v6)

            def gather(half, buf, id_, v5, gfree):
                toks = []
                for h in range(8):
                    nm = f"g{half}{h}"
                    if nm not in dsem:
                        dsem[nm] = [sem(nm), 0]
                    toks.append(G.dma([v5, gfree[h]], dsem[nm], nc.gpsimd.indirect_dma_start, out=buf[:, h, :],
                                      out_offset=None, in_=d[f"tab{half}"],
                                      in_offset=bass.IndirectOffsetOnAxis(ap=id_.ap[:, h:h + 1], axis=0),
                                      bounds_check=4095, oob_is_err=False))
                return toks

            def peer():
                q = {"mx": None, "mif": None}
                last = {"hg": None, "x": None, "hT": None}
                rt = {}
                for t in range(2):
                    yield from route(t, q)
                    rt[t] = q["out"]
                ka = gather(0, GA, rt[0][0], rt[0][2], [ws_used] * 8)
                kb = gather(1, GB, rt[0][0], rt[0][2], [None] * 8)
                rt[0][0].release(*ka, *kb)

                def first_half(t):
                    ts = slice(t * 128, (t + 1) * 128)
                    p = psk.take()
                    t_ = transposes([g1, p.free], [(p.ap[:, k * 128:(k + 1) * 128], xn[:, k, ts]) for k in range(2)],
                                    ident[:, :])
                    xa = A.do([t_, last["x"]], act, xt_[:, :], p.ap[:, 0:256], ACT.Copy)
                    p.release(xa)
                    ph_ = psk.take()
                    th = group([w_p, ph_.free], chain(ph_.ap[:, :], [(xn[:, k, ts], Pi[:, k, :]) for k in range(2)]))
                    return xa, ph_, th

                def finish(t, hT, dg):
                    ts = slice(t * 128, (t + 1) * 128)
                    p = psk.take()
                    mms = []
                    for m in range(2):
                        ms = slice(m * 128, (m + 1) * 128)
                        mms += chain(p.ap[:, ms], [(Po[:, k, ms], hgT[:, k * 128:(k + 1) * 128]) for k in range(4)]
                                     + [(oacc[:, ms], ident[:, :])])
                    t_ = group([hT, dg, p.free], mms)
                    last["hT"] = last["o"] = t_
                    v_ = xw[t // 4] = V.do([t_, xw[t // 4]], nvt, xT[:, :, ts], xT[:, :, ts], p.ap[:, 0:256].rearrange("p (m t) -> p m t", m=2),
                              ALU.add)
                    p.release(v_)
                    fdone.append(v_)

                last["o"] = last["fh"] = None
                junk = [[hacc, None], [jk, None]]
                fh = first_half(0)
                fin = None
                for t in range(NT):
                    gt_, v6 = rt[t][1], rt[t][3]
                    xa, ph_, th = fh
                    for h in range(8):
                        jt = junk[h % 2]
                        v_ = jt[1] = V.do([xa, ka[h], jt[1], last["fh"]], nc.vector.tensor_tensor_reduce,
                                          out=jt[0][:, 0:256], in0=xt_[:, :], in1=GA[:, h, 0:256], scale=1.0,
                                          scalar=0.0, op0=ALU.mult, op1=ALU.add, accum_out=lin[:, h:h + 1])
                        if h == 3:
                            yield
                    last["x"] = v_
                    yield
                    v_ = V.do([v_, v6], nvt, lin[:, 0:8], lin[:, 0:8], gt_.ap[:, :], ALU.mult)
                    src = ph_.ap[:, :]
                    used = []
                    for h in range(8):
                        v_ = V.do([v_, th], stt, out=hacc[:, :], in0=GA[:, h, 256:768], scalar=lin[:, h:h + 1],
                                  in1=src, op0=ALU.mult, op1=ALU.add)
                        src = hacc[:, :]
                        used.append(v_)
                        if h == 0:
                            ph_.release(v_)
                        if h % 2:
                            yield
                    if t + 1 < NT:
                        ka = gather(0, GA, rt[t + 1][0], rt[t + 1][2], used)
                    a_ = A.do([v_, last["hg"]], act, hg[:, :], hacc[:, :], ACT.Gelu)
                    yield
                    rg = route(t + 2, q) if t + 2 < NT else iter(range(4))
                    for i, _ in enumerate(rg):
                        yield
                        if i == 1 and fin is not None:
                            finish(*fin)
                            yield
                    if t + 2 < NT:
                        rt[t + 2] = q["out"]
                    p = psk.take()
                    t_ = transposes([a_, p.free], [(p.ap[:, k * 128:(k + 1) * 128], hg[:, k * 128:(k + 1) * 128])
                                                   for k in range(4)], ident[:, :])
                    hT = A.do([t_, last["hT"]], act, hgT[:, :], p.ap[:, :], ACT.Copy)
                    p.release(hT)
                    for h in range(8):
                        jt = junk[h % 2]
                        v_ = jt[1] = V.do([a_, kb[h], jt[1]], nc.vector.tensor_tensor_reduce, out=jt[0][:, :],
                                          in0=hg[:, :], in1=GB[:, h, 0:512], scale=1.0, scalar=0.0, op0=ALU.mult,
                                          op1=ALU.add, accum_out=lin[:, 8 + h:9 + h])
                        if h % 2:
                            yield
                    last["hg"] = v_
                    v_ = last["fh"] = V.do([v_], nvt, lin[:, 8:16], lin[:, 8:16], gt_.ap[:, :], ALU.mult)
                    gt_.release(v_)
                    v_ = V.do([v_, last["o"]], nvs, oacc[:, :], GB[:, 0, 512:768], lin[:, 8:9], None, ALU.mult)
                    used = [v_]
                    for h in range(1, 8):
                        v_ = V.do([v_], stt, out=oacc[:, :], in0=GB[:, h, 512:768], scalar=lin[:, 8 + h:9 + h],
                                  in1=oacc[:, :], op0=ALU.mult, op1=ALU.add)
                        used.append(v_)
                        if h % 3 == 2:
                            yield
                    fin = (t, hT, v_)
                    if t + 1 < NT:
                        kb = gather(1, GB, rt[t + 1][0], rt[t + 1][2], used)
                        rt[t + 1][0].release(*ka, *kb)
                        fh = first_half(t + 1)
                    yield
                finish(*fin)

            interleave((mamba(), 4.2), (peer(), 1.0))
            barrier()
            ph.close()
            return [[done[n], fdone[4 * n + 3]] for n in range(NB)]

        def layer2(ready):
            ph = ExitStack()
            sb = alloc(ph)
            Wr = sb("rW", [128, 2, 256])
            W1 = sb("rW1", [128, 2, 1024])
            W2 = sb("rW2", [128, 8, 256])
            vec = sb("vec2", [128, 32])
            for t_, n_ in ((Wr, "rWr"), (W1, "rW1"), (W2, "rW2")):
                w_r = dma([], "w2r", t_[:, :, :], d[n_])
            w_r = dma([], "w2r", vec[:, :], d["vec2"])
            K0, K1, K2 = (sb(n_, sh_, F32R) for n_, sh_ in (("K0", [128, 2, 1024]), ("K1", [128, 8, 1024]),
                                                           ("K2", [128, 8, 256])))
            eh = sb("reh", [128, 4, BW])
            e_, h_ = eh[:, 0:2, :], eh[:, 2:4, :]
            raw = eh[:, :, :].rearrange("p a b -> p (a b)").bitcast(U8).rearrange("p (a b) -> p a b", a=8)
            b_r, l1s, l1b, l2s, l2b = (vec[:, 2 * i:2 * i + 2] for i in range(5))
            b1, b2, sc = vec[:, 10:18], vec[:, 18:20], vec[:, 20:23]
            psr = Ring(PS[0:2])
            psb = Ring(PS[2:4])
            racc = Ring(PS[4:6])
            bacc_ = Ring(PS[6:8])
            big = Ring([sb(f"bh{i}", [128, 2, BW]) for i in range(2)])
            fa = sb("fa", [128, 5, BW])
            ft = Ring([fa[:, i, :] for i in range(3)])
            ac = Ring([fa[:, i, :] for i in (3, 4)])
            lnr = layer_norm_all(ready, Ring(big.bufs + [fa[:, 0:2, :], fa[:, 2:4, :]]), psr)
            for ring in (big, ft, ac):
                ring.free = [[lnr[-1]] for _ in ring.bufs]
            wr = dma([], "w2k0", raw[:, 0:4, :], d["k0"])
            w_k0 = None
            for k in range(2):
                for hf in range(2):
                    f_ = ft.take()
                    g_ = V.do([wr, f_.free], nvs, f_.ap[:, :], raw[:, 2 + k, hf * 512:(hf + 1) * 512], 2.0, None,
                              ALU.mult)
                    w_k0 = V.do([g_], stt, out=K0[:, k, hf * 512:(hf + 1) * 512],
                                in0=raw[:, k, hf * 512:(hf + 1) * 512], scalar=2.0, in1=f_.ap[:, :], op0=ALU.mult,
                                op1=ALU.subtract)
                    f_.release(w_k0)
            wr = dma([w_k0], "w2k1", raw[:, :, :], d["k1"])
            w_k1 = V.do([wr, w_k0], nvs, K1[:, :, :], raw[:, :, :], 2.0, -1.0, ALU.mult, ALU.add)
            wr = dma([w_k1], "w2k2", raw[:, 0:2, :].rearrange("p a b -> p (a b)"), d["k2"])
            w_k2 = V.do([wr], nvs, K2[:, :, :], raw[:, 0:2, :].rearrange("p a (b c) -> p (a b) c", b=4), 2.0, -1.0,
                        ALU.mult, ALU.add)
            s2 = sb("s2c", [128, 2])
            c_s2 = V.do([w_r], nvs, s2[:, :], sc[:, 0:2], 2.0, None, ALU.mult)
            half = sb("half", [128, 1])
            c_half = V.do([], nc.vector.memset, half[:, :], 0.5)
            sig = [e_[:, i, :] for i in range(2)]
            rl = sb("rl", [128, 2])
            done, fdone = [], []

            def reten():
                s = {"rl": None, "e": w_k2, "h": [w_k2]}
                for n in range(NB):
                    for m in range(2):
                        p = psr.take()
                        t_ = group([lnr[n], w_r, p.free], chain(p.ap[:, :], [(Wr[:, k, m * 128:(m + 1) * 128],
                                                                              xs(n, k)) for k in range(2)]))
                        a_ = A.do([t_, s["e"]], act, sig[m], p.ap[:, :], ACT.Sigmoid, bias=b_r[:, m:m + 1])
                        p.release(a_)
                        init = 0.0 if n % 4 == 0 else rl[:, m:m + 1]
                        v_ = V.do([a_, c_half, s["rl"]], nc.vector.tensor_tensor_scan, sig[m],
                                  half[:, 0:1].broadcast_to([128, BW]), sig[m], init, ALU.mult, ALU.add)
                        l_ = V.do([v_], nc.vector.tensor_copy, rl[:, m:m + 1], sig[m][:, BW - 1:BW])
                        et = V.do([v_, l_], stt, out=e_[:, m, :], in0=sig[m], scalar=0.5, in1=xs(n, m),
                                  op0=ALU.mult, op1=ALU.add)
                    s["rl"] = l_
                    yield
                    R = []
                    yield from norm_stages(e_[:, :, :], et, h_[:, :, :], R, big, psr, (l1s, l1b), dst_free=s["h"])
                    s["e"] = R[0]
                    hr = R[0]
                    yield
                    acc = [racc.take(), racc.take()]
                    pend = None
                    for m in range(9):
                        if m < 8:
                            p = psr.take()
                            t_ = group([hr, p.free], chain(p.ap[:, :], [(W1[:, k, m * 128:(m + 1) * 128],
                                                                         h_[:, k, :]) for k in range(2)]))
                            g_ = ac.take()
                            a_ = A.do([t_, g_.free], act, g_.ap[:, :], p.ap[:, :], ACT.Gelu_apprx_tanh,
                                      bias=b1[:, m:m + 1])
                            p.release(a_)
                            yield
                        if m > 0:
                            ta = group([pend[1], acc[0].free, acc[1].free],
                                       [(acc[o].ap[:, :], W2[:, m - 1, o * 128:(o + 1) * 128], pend[0].ap[:, :],
                                         m == 1, m == 8) for o in range(2)])
                            pend[0].release(ta)
                        pend = (g_, a_)
                    for m in range(2):
                        et = V.do([ta, s["e"]], stt, out=e_[:, m, :], in0=acc[m].ap[:, :], scalar=b2[:, m:m + 1],
                                  in1=h_[:, m, :], op0=ALU.add, op1=ALU.add)
                        acc[m].release(et)
                    yield
                    R = []
                    yield from norm_stages(e_[:, :, :], et, h_[:, :, :], R, big, psr, (l2s, l2b), dst_free=[et])
                    s["e"] = R[0]
                    g_ = xw[n] = V.do([R[0], xw[n]], nvt, xT[:, :, n * BW:(n + 1) * BW], xT[:, :, n * BW:(n + 1) * BW], h_[:, :, :],
                              ALU.add)
                    s["h"] = [g_]
                    done.append(g_)
                    yield

            xa = sb("xa", [128, 2, 2, BW], F32R)
            f1 = sb("f1", [128, 2, 8, BW], F32R)
            f2 = Ring([sb(f"f2{i}", [128, 2, BW], F32R) for i in range(2)])

            def split(src, r_src, hi, lo, free):
                v_ = V.do([r_src, *free], nc.vector.tensor_copy, hi, src)
                return v_, G.do([v_], nc.gpsimd.tensor_tensor, lo, src, hi.bitcast(F32), ALU.subtract)

            def two(w, hi, lo):
                return [(w, hi), (w, lo)]

            def binary():
                s = {"xa": [], "f1": []}
                for n in range(NB):
                    _, xr = split(xn[:, :, n * BW:(n + 1) * BW], lnr[n], xa[:, 0, :, :], xa[:, 1, :, :], s["xa"])
                    for m in range(8):
                        p = psb.take()
                        ms = slice(m * 128, (m + 1) * 128)
                        t_ = group([xr, w_k0, p.free], chain(p.ap[:, :], [
                            q for k in range(2) for q in two(K0[:, k, ms], xa[:, 0, k, :], xa[:, 1, k, :])]))
                        f_ = ft.take()
                        a1 = A.do([t_, c_s2, f_.free], act, f_.ap[:, :], p.ap[:, :], ACT.Relu, scale=s2[:, 0:1])
                        p.release(a1)
                        v1, g1_ = split(f_.ap[:, :], a1, f1[:, 0, m, :], f1[:, 1, m, :], s["f1"])
                        f_.release(g1_, v1)
                        if m % 2:
                            yield
                    s["xa"] = [t_]
                    acc = [bacc_.take(), bacc_.take()]
                    pend = None
                    for m in range(9):
                        if m < 8:
                            p = psb.take()
                            ms = slice(m * 128, (m + 1) * 128)
                            t_ = group([g1_, w_k1, p.free], chain(p.ap[:, :], [
                                q for k in range(8) for q in two(K1[:, k, ms], f1[:, 0, k, :], f1[:, 1, k, :])]))
                            f_, g_ = ft.take(), f2.take()
                            a1 = A.do([t_, f_.free], act, f_.ap[:, :], p.ap[:, :], ACT.Relu, scale=s2[:, 1:2])
                            p.release(a1)
                            v1, gt = split(f_.ap[:, :], a1, g_.ap[:, 0, :], g_.ap[:, 1, :], g_.free)
                            f_.release(gt, v1)
                            yield
                        if m > 0:
                            ta = group([pend[1], w_k2, acc[0].free, acc[1].free],
                                       [(acc[o].ap[:, :], K2[:, m - 1, o * 128:(o + 1) * 128], pend[0].ap[:, i, :],
                                         m == 1 and i == 0, m == 8 and i == 1) for o in range(2) for i in range(2)])
                            pend[0].release(ta)
                        pend = (g_, gt)
                    s["f1"] = [t_]
                    for m in range(2):
                        v_ = xw[n] = V.do([ta, xw[n]], stt, out=blk(xT, m, n), in0=acc[m].ap[:, :], scalar=sc[:, 2:3],
                                  in1=blk(xT, m, n), op0=ALU.mult, op1=ALU.add)
                        acc[m].release(v_)
                    fdone.append(v_)
                    yield

            interleave((reten(), 1.0), (binary(), 1.2))
            barrier()
            ph.close()
            return [[done[n], fdone[n]] for n in range(NB)]

        def layer3(ready):
            ph = ExitStack()
            sb = alloc(ph)
            WoP = sb("aWo", [128, 4, 256])
            WQ, WK = sb("WQr", [128, 2, 8, 128]), sb("WKr", [128, 2, 8, 128])
            Wvn = sb("aWv", [128, 2, 256])
            alf = sb("alf", [128, 2])
            negb = sb("negb", [128, 2, 128], BF16)
            selS = sb("selS", [128, 4, 32])
            orow = sb("orow", [1, 128 + BW], BF16)
            ph2 = ExitStack()
            sb2 = alloc(ph2)
            Wqn, Wkn = sb2("aWq", [128, 2, 256]), sb2("aWk", [128, 2, 256])
            th4 = [sb2(f"th{i}", [128, 2, 256]) for i in range(4)]
            for t_, n_ in ((Wqn, "aWq"), (Wkn, "aWk"), (Wvn, "aWv")):
                w_a = dma([], "w3a", t_[:, :, :], d[n_])
            c0 = V.do([], nc.vector.memset, WoP[:, :, :], 0.0)
            for j in range(4):
                w_o = dma([c0], "w3o", WoP[32 * j:32 * j + 16, :, :], d["aWo"][:, j, :, :])
            for i, n_ in enumerate(("theta", "theta_noise", "phi", "phi_noise")):
                w_t = dma([], "w3t", th4[i][:, :, :], d[n_])
            psx = Ring(PS[0:3])
            big = Ring([sb2(f"bi{i}", [128, 2, BW]) for i in range(4)])
            lnr = layer_norm_all(ready, big, psx)
            for w_, r_, sc_ in ((Wqn, WQ, 0.25), (Wkn, WK, 1.0)):
                g_ = G.do([], nc.gpsimd.memset, r_[:, :, :, :], 0.0)
                for o_ in (0, 16, 48):
                    for k in range(2):
                        c_rep = V.do([g_, w_a], nvs,
                                     r_[:, k, :, :].rearrange("p a (b c) -> p (a b) c", b=2)[:, :, o_:o_ + 16],
                                     w_[:, k, :].rearrange("p (h c) -> p h c", c=16), sc_, None, ALU.mult)
            TR = [sb2(f"TR{i}", [128, 2, 256]) for i in range(2)]
            ki = sb2("ki", [128, 2, 256], I32)
            kf = sb2("kf", [128, 2, 2, 256])
            v_ = kf_ = None
            for i, (a0, b0, off) in enumerate(((0, 1, 0.25), (2, 3, 0.0))):
                t0, t1 = th4[a0][:, :, :], th4[b0][:, :, :]
                v_ = V.do([w_t, v_], nvt, t0, t0, t1, ALU.add)
                v_ = V.do([v_], nvs, t1, t0, 0.15915494309189535, off, ALU.mult, ALU.add)
                v_ = V.do([v_], nc.vector.tensor_copy, ki[:, :, :], t1)
                v_ = V.do([v_, kf_], nc.vector.tensor_copy, kf[:, 0, :, :], ki[:, :, :])
                v_ = V.do([v_], nvt, t1, t1, kf[:, 0, :, :], ALU.subtract)
                u_ = V.do([v_], nvs, kf[:, 1, :, :], t1, -0.5, -1.0, ALU.is_lt, ALU.mult)
                w_ = V.do([v_], nvs, t1, t1, 0.5, None, ALU.is_gt)
                v_ = V.do([w_, u_], nvt, t1, t1, kf[:, 1, :, :], ALU.add)
                v_ = kf_ = V.do([v_], nvt, t1, t1, kf[:, 0, :, :], ALU.add)
                if off:
                    v_ = V.do([v_], nvs, t0, t0, 1.5707963267948966, None, ALU.add)
                v_ = V.do([v_], stt, out=t0, in0=t1, scalar=-6.28125, in1=t0, op0=ALU.mult, op1=ALU.add)
                v_ = V.do([v_], stt, out=t0, in0=t1, scalar=-0.0019353071795864769, in1=t0, op0=ALU.mult,
                          op1=ALU.add)
                v_ = V.do([v_], nvs, t0, t0, 3.1415925, -3.1415925, ALU.min, ALU.max)
                c_tr = A.do([v_], act, TR[i][:, :, :], t0, ACT.Sin)
            tmp = Ring([sb2(f"tn{i}", [128, BW]) for i in range(4)])
            fd = {}
            for n in range(NB):
                for m in range(2):
                    ms = slice(m * 128, (m + 1) * 128)
                    t2 = []
                    for i in range(2):
                        p = psx.take()
                        t_ = group([lnr[n], c_tr, p.free], chain(p.ap[:, :], [(TR[i][:, k, ms], xs(n, k))
                                                                              for k in range(2)]))
                        s_ = tmp.take()
                        a_ = A.do([t_, s_.free], act, s_.ap[:, :], p.ap[:, :], ACT.Square)
                        p.release(a_)
                        t2.append((s_, a_))
                    (s0, a0), (s1, a1) = t2
                    g_ = G.do([a0, a1], nc.gpsimd.tensor_tensor, s0.ap[:, :], s0.ap[:, :], s1.ap[:, :], ALU.add)
                    s1.release(g_)
                    a_ = A.do([g_], act, s0.ap[:, :], s0.ap[:, :], ACT.Sqrt)
                    v_ = xw[n] = V.do([a_, xw[n]], nvt, blk(xT, m, n), blk(xT, m, n), s0.ap[:, :], ALU.add)
                    s0.release(v_)
            mk = None
            mf = tmp.take().ap[:, 0:128]
            for i, (cm, st_) in enumerate(((1, -1), (-1, 1))):
                g_ = G.do([mk, v_], nc.gpsimd.memset, mf, 0.0)
                g_ = G.do([g_], nc.gpsimd.affine_select, out=mf, in_=mf, compare_op=ALU.is_ge, fill=NEG, base=0,
                          pattern=[[st_, 128]], channel_multiplier=cm)
                mk = V.do([g_], nc.vector.tensor_copy, negb[:, i, :], mf)
            for i, lo in enumerate((48, 16)):
                V.do([], nc.vector.tensor_reduce, alf[:, i:i + 1],
                     ident[:, :].rearrange("p (h c) -> p h c", h=2)[:, :, lo:lo + 16], AX.XY, ALU.add, negate=True)
            V.do([], nc.vector.tensor_copy, selS[:, :, :],
                 ident[:, :].rearrange("p (j c) -> p j c", j=4)[:, :, 16:17].broadcast_to([128, 4, 32]))
            v_ = V.do([], nc.vector.memset, orow[:, :], 1.0)
            v_ = V.do([v_], nc.vector.memset, orow[:, 0:128], 0.0)
            for o_ in (32, 96):
                V.do([v_], nc.vector.memset, orow[:, o_:o_ + 1], 1.0)
            barrier()
            ph2.close()

            NQ = 4
            QS = [sb(f"QS{i}", [128, 2, SEQ], F32R) for i in range(2)]
            KS = [sb(f"KS{i}", [128, 2, SEQ], F32R) for i in range(2)]
            Va = sb("Va", [128, 16, 288])
            Pr = Ring([sb(f"P{i}", [128, 2, BW]) for i in range(3)])
            hi = Ring([sb(f"hi{i}", [128, BW], F32R) for i in range(2)])
            osb, On = sb("osb", [128, BW]), sb("On", [128, BW])
            pm = sb("pm", [128, 4, 16, 4])
            mxs = sb("mxs", [128, 4, 16], BF16)
            c_pm = V.do([], nc.vector.memset, pm[:, :, :, :], -3.0e38)
            c_va = V.do([], nc.vector.memset, Va[:, :, :], 1.0)
            S2 = Ring([(PS[3], PS[4]), (PS[5], PS[6])])
            po = Ring([PS[7]])
            qfree, kfree = [[], []], [[], []]
            Qr, Kr = {}, {}
            sv = {"va": [c_va], "mxs": None, "pm": [c_pm], "o": None, "on": None}
            xdone = {}

            def vproj(b):
                for kt in range(16):
                    ts = slice(b * SEQ + kt * 128, b * SEQ + (kt + 1) * 128)
                    p = psx.take()
                    t_ = group([p.free], chain(p.ap[:, 0:256], [(xn[:, k, ts], Wvn[:, k, :]) for k in range(2)]))
                    v_ = V.do([t_, *sv["va"]], nc.vector.tensor_copy,
                              Va[:, kt, 0:272].rearrange("p (h c) -> p h c", c=17)[:, :, 0:16],
                              p.ap[:, 0:256].rearrange("p (h c) -> p h c", c=16))
                    p.release(v_)
                    yield
                sv["var"] = v_

            def prep(b, g):
                i = (b * 4 + g) % 2
                for W_, S_, col, fr in ((WQ, QS, 0, qfree), (WK, KS, 1, kfree)):
                    for pr in range(2):
                        for n in range(NQ):
                            bs = slice(b * SEQ + n * BW, b * SEQ + (n + 1) * BW)
                            p = psx.take()
                            mms = chain(p.ap[:, :], [(W_[:, k, 2 * g + pr, :], xn[:, k, bs]) for k in range(2)])
                            if col:
                                mms[-1] = mms[-1][:4] + (False,)
                                mms.append((p.ap[:, :], orow[:, 0:128], orow[:, 128:128 + BW], False, True))
                            t_ = group([p.free], mms)
                            h_ = hi.take()
                            a_ = A.do([t_, h_.free], act, h_.ap[:, :], p.ap[:, :], ACT.Copy)
                            s_ = V.do([a_, *fr[i]], stt, out=S_[i][:, pr, n * BW:(n + 1) * BW],
                                      in0=h_.ap[:, :].bitcast(F32), scalar=alf[:, col:col + 1], in1=p.ap[:, :],
                                      op0=ALU.mult, op1=ALU.add)
                            h_.release(s_)
                            p.release(s_)
                            yield
                Q, K = QS[i], KS[i]
                for hd in range(4):
                    pr, r0 = hd // 2, 64 * (hd % 2)
                    for qt in range(16):
                        for c in range(qt // 4 + 1):
                            w = min(512, (qt + 1) * 128 - c * 512)
                            p = psx.take()
                            mms = [(p.ap[:, 0:w], Q[r0:r0 + 64, pr, qt * 128:(qt + 1) * 128],
                                    K[r0:r0 + 64, pr, c * 512:c * 512 + w], True, c < qt // 4)]
                            if c == qt // 4:
                                mms.append((p.ap[:, w - 128:w], identb[:, :], negb[:, 0, :], False, True))
                            t_ = group([s_, p.free], mms)
                            v_ = V.do([t_, *sv["pm"]], nc.vector.tensor_reduce, pm[:, hd, qt, c:c + 1],
                                      p.ap[:, 0:w], AX.X, ALU.max)
                            p.release(v_)
                            yield
                m_ = V.do([v_, sv["mxs"]], nc.vector.tensor_reduce, mxs[:, :, :], pm[:, :, :, :], AX.X, ALU.max,
                          negate=True)
                sv["pm"] = [m_]
                for pr in range(2):
                    for n in range(NQ):
                        p = psx.take()
                        mms = [(p.ap[32 + 64 * hh:33 + 64 * hh, c * 128:(c + 1) * 128],
                                mxs[:, 2 * pr + hh, 4 * n + c:4 * n + c + 1], identb[:, :], True, True)
                               for hh in range(2) for c in range(4)]
                        t_ = group([m_, p.free], mms)
                        for hh in range(2):
                            r = 32 + 64 * hh
                            q_ = A.do([t_], act, Q[r:r + 1, pr, n * BW:(n + 1) * BW], p.ap[r:r + 1, :], ACT.Copy)
                        p.release(q_)
                        yield
                sv["mxs"] = t_
                Qr[(b, g)] = q_

            def main(b, g):
                i = (b * 4 + g) % 2
                Q, K = QS[i], KS[i]
                for n in range(NQ):
                    o_ = po.take()
                    nk = 4 * n + 4
                    pend = None
                    for kt in range(nk + 1):
                        if kt < nk:
                            off = max(0, (kt - 4 * n) * 128)
                            cur = []
                            for pr in range(2):
                                s2, P_ = S2.take(), Pr.take()
                                mms = []
                                for hh in range(2):
                                    rs = slice(64 * hh, 64 * hh + 64)
                                    diag = kt >= 4 * n
                                    mms.append((s2.ap[hh][:, off:BW], K[rs, pr, kt * 128:(kt + 1) * 128],
                                                Q[rs, pr, n * BW + off:(n + 1) * BW], True, not diag))
                                if diag:
                                    for hh in range(2):
                                        mms.append((s2.ap[hh][:, off:off + 128], identb[:, :], negb[:, 1, :], False,
                                                    True))
                                t_ = group([Qr[(b, g)], s2.free], mms)
                                for hh in range(2):
                                    a_ = A.do([t_, P_.free], act, P_.ap[:, hh, off:BW], s2.ap[hh][:, off:BW],
                                              ACT.Exp)
                                s2.release(a_)
                                cur.append((P_, a_))
                                yield
                                if pr == 0 and pend is not None:
                                    tp = pv(g, pend, o_, nk)
                                    pend = None
                                    yield
                            pend = (kt, off, cur)
                    tp = pv(g, pend, o_, nk)
                    a_ = A.do([tp, sv["o"]], act, osb[:, :], o_.ap[:, :], ACT.Copy)
                    o_.release(a_)
                    yield
                    p = psx.take()
                    t_ = group([a_, p.free], [(p.ap[:, :], selS[:, :, :].rearrange("p a b -> p (a b)"), osb[:, :],
                                               True, True)])
                    v_ = V.do([t_, sv["on"]], nc.vector.reciprocal, On[:, :], p.ap[:, :])
                    p.release(v_)
                    v_ = V.do([v_], nvt, On[:, :], On[:, :], osb[:, :], ALU.mult)
                    sv["o"] = v_
                    bs = slice(b * SEQ + n * BW, b * SEQ + (n + 1) * BW)
                    yield
                    for m in range(2):
                        p = psx.take()
                        t_ = group([v_, p.free], [(p.ap[:, :], WoP[:, g, m * 128:(m + 1) * 128], On[:, :], True,
                                                   True)])
                        x_ = xw[4 * b + n] = V.do([t_, xw[4 * b + n]], nvt, xT[:, m, bs], xT[:, m, bs], p.ap[:, :], ALU.add)
                        p.release(x_)
                    sv["on"] = t_
                    xdone[4 * b + n] = x_
                    yield
                qfree[i] = kfree[i] = [t_]
                sv["va"] = [t_]

            def pv(g, pend, o_, nk):
                kt, off, cur = pend
                mms = []
                for hd in range(4):
                    P_ = cur[hd // 2][0]
                    h = 4 * g + hd
                    mms.append((o_.ap[32 * hd:32 * hd + 32, off:BW], Va[:, kt, h * 17:h * 17 + 32],
                                P_.ap[:, hd % 2, off:BW], kt == 0, kt == nk - 1))
                tp = group([cur[0][1], cur[1][1], sv["var"]] + (o_.free if kt == 0 else []), mms)
                for P_, _ in cur:
                    P_.release(tp)
                return tp

            order = [(b, g) for b in range(2) for g in range(4)]
            for _ in vproj(0):
                pass
            for _ in prep(0, 0):
                pass
            for j, (b, g) in enumerate(order):
                if (b, g) == (1, 0):
                    for _ in vproj(1):
                        pass
                if j + 1 < len(order):
                    interleave((main(b, g), 1.34), (prep(*order[j + 1]), 1.0))
                else:
                    for _ in main(b, g):
                        pass
            ph.close()
            return [xdone[n] for n in range(NB)]

        ready = xload
        if FIRST <= 1 <= LAYERS:
            ready = layer0(ready)
        if FIRST <= 2 <= LAYERS:
            ready = layer1(ready)
        if FIRST <= 3 <= LAYERS:
            ready = layer2(ready)
        if FIRST <= 4 <= LAYERS:
            ready = layer3(ready)
        for n in range(NB):
            tok = dma([ready[n]], "out", out[:, :, n * BW:(n + 1) * BW], xT[:, :, n * BW:(n + 1) * BW])
        SP.wait(tok)

        block = ctx.enter_context(nc.Block())

        @block.sync
        def _(eng):
            SP.emit(eng)

        @block.tensor
        def _(eng):
            PE.emit(eng)

        @block.vector
        def _(eng):
            V.emit(eng)

        @block.scalar
        def _(eng):
            A.emit(eng)

        @block.gpsimd
        def _(eng):
            G.emit(eng)


def layout(i):
    import numpy as np

    def c(a):
        return np.ascontiguousarray(a)

    def wt(a):
        return c(a.reshape(-1, 128, a.shape[-1]).transpose(1, 0, 2))

    def pv(*vs):
        cols = [v.reshape(-1, 128).T for v in vs]
        n = sum(x.shape[1] for x in cols)
        return cols, n

    def vec(width, *vs):
        cols, n = pv(*vs)
        cols.append(np.zeros((128, width - n), np.float32))
        return c(np.concatenate(cols, axis=1))

    def ex(a):
        e, k, o = a.shape
        return c(a.reshape(e, k // 128, 128, o).transpose(2, 0, 1, 3))

    g = {k: np.asarray(v) for k, v in i.items()}
    r = {}
    r["x"] = c(g["L0_attn_x"].reshape(T, 2, 128).transpose(2, 1, 0))
    for n, s in (("Wq", "L0_attn_Wq"), ("Wk", "L0_attn_Wk"), ("Wv", "L0_attn_Wv"), ("Wg", "L0_attn_Wg"),
                 ("Wgk1", "L0_attn_Wgk1"), ("Wo", "L0_attn_Wo"), ("Wr", "L0_ffn_Wr"), ("mWi", "L1_attn_W_in"),
                 ("mWd", "L1_attn_Wd"), ("mWo", "L1_attn_W_out"), ("rWr", "L2_attn_W_ret"), ("rW1", "L2_attn_W1"),
                 ("rW2", "L2_attn_W2"), ("theta", "L3_ffn_theta"), ("theta_noise", "L3_ffn_theta_noise"),
                 ("phi", "L3_ffn_phi"), ("phi_noise", "L3_ffn_phi_noise")):
        r[n] = wt(g[s])
    r["Wgk2"] = c(g["L0_attn_Wgk2"])
    r["vec0"] = vec(3, g["L0_attn_bgk2"], g["L0_attn_g_norm_weight"])
    r["F1"], r["F3"], r["F2"] = ex(g["L0_ffn_W1"]), ex(g["L0_ffn_W3"]), ex(g["L0_ffn_W2"])
    r["vec1"] = vec(32, g["L1_attn_ln_gamma"], g["L1_attn_ln_beta"], g["L1_attn_conv_b"], g["L1_attn_bd"],
                    g["L1_attn_D_vec"])
    r["mcw"] = c(g["L1_attn_conv_w"].reshape(4, 128, 4).transpose(1, 0, 2))
    r["mA"] = c(g["L1_attn_A_log"].reshape(16, 1))
    r["mB"] = wt(c(g["L1_attn_B_mat"].T))
    r["mC"] = c(g["L1_attn_C_mat"].T)
    r["pWq"] = c(g["L1_ffn_Wq"].reshape(16, 128, 256).transpose(1, 0, 2))
    r["keys"] = c(g["L1_ffn_keys"].transpose(3, 2, 0, 1).reshape(128, 16, 128))
    r["pWi"] = wt(c(g["L1_ffn_W_in"].T))
    r["pWo"] = wt(c(g["L1_ffn_W_out"].T))
    r["tab0"] = c(np.concatenate([g["L1_ffn_in_a"], g["L1_ffn_in_b"]], axis=1))
    r["tab1"] = c(np.concatenate([g["L1_ffn_out_a"], g["L1_ffn_out_b"]], axis=1))
    sc = [np.broadcast_to(g[f"L2_ffn_s{n}"], (128,)) for n in range(3)]
    r["vec2"] = vec(32, g["L2_attn_b_ret"], g["L2_attn_ln1_scale"], g["L2_attn_ln1_bias"], g["L2_attn_ln2_scale"],
                    g["L2_attn_ln2_bias"], g["L2_attn_b1"], g["L2_attn_b2"], *sc)
    for n in ("k0", "k1", "k2"):
        r[n] = wt(g[f"L2_ffn_{n}"])
    r["k2"] = r["k2"].reshape(128, -1)
    for n, s in (("aWq", "q"), ("aWk", "k"), ("aWv", "v")):
        r[n] = wt(c(g[f"L3_attn_{s}_proj_weight"].T))
    r["aWo"] = c(g["L3_attn_o_proj_weight"].T.reshape(4, 4, 16, 256).transpose(2, 1, 0, 3))
    return r


def kernel(**inputs):
    import numpy as np
    import concourse.bacc as bacc
    from concourse.bass_utils import run_bass_kernel_spmd

    arrays = layout(inputs)
    nc = bacc.Bacc("TRN2", target_bir_lowering=False, num_devices=1)
    d = {n: nc.dram_tensor(f"in_{n}", a.shape, mybir.dt.from_np(a.dtype), kind="ExternalInput").ap()
         for n, a in arrays.items()}
    out = nc.dram_tensor("out_0", (128, 2, T), F32, kind="ExternalOutput").ap()
    build(nc, d, out)
    r = run_bass_kernel_spmd(nc, [{f"in_{n}": a for n, a in arrays.items()}], core_ids=[0])
    y = r.results[0]["out_0"]
    return np.ascontiguousarray(y.transpose(2, 1, 0)).reshape(2, SEQ, 256)
```

```python
from contextlib import ExitStack

import concourse.bass as bass
from concourse import mybir

ALU = mybir.AluOpType
ACT = mybir.ActivationFunctionType
F32 = mybir.dt.float32
F32R = mybir.dt.float32r
BF16 = mybir.dt.bfloat16
U32 = mybir.dt.uint32
I32 = mybir.dt.int32
U8 = mybir.dt.uint8
AX = mybir.AxisListType

T = 4096
NB = 8
BW = 512
SEQ = 2048
NEG = -1.0e30
EPS = 1e-5


class Queue:

    def __init__(self, sem):
        self.sem = sem
        self.n = 0
        self.items = []
        self.seen = {}

    def wait(self, *toks):
        for t in toks:
            if t is None:
                continue
            if isinstance(t, list):
                self.wait(*t)
                continue
            sem, val = t
            if self.seen.get(id(sem), 0) < val:
                self.seen[id(sem)] = val
                self.items.append((None, sem, val))

    def do(self, after, fn, *args, **kw):
        self.wait(*after)
        self.n += 1
        self.items.append((fn, args, kw, self.sem, 1))
        return (self.sem, self.n)

    def quiet(self, fn, *args, **kw):
        self.items.append((fn, args, kw, None, 0))

    def dma(self, after, sem, fn, *args, **kw):
        self.wait(*after)
        self.items.append((fn, args, kw, sem[0], 16))
        sem[1] += 16
        return (sem[0], sem[1])

    def last(self):
        return (self.sem, self.n) if self.n else None

    def emit(self, eng):
        for it in self.items:
            if it[0] is None:
                eng.wait_ge(it[1], it[2])
            else:
                ins = it[0](*it[1], **it[2])
                if it[3] is not None:
                    ins.then_inc(it[3], it[4])


class Slot:
    def __init__(self, ring, i):
        self.ring, self.i = ring, i
        self.ap = ring.bufs[i]
        self.free = ring.free[i]

    def release(self, *toks):
        assert self.ring.held[self.i]
        self.ring.held[self.i] = False
        self.ring.free[self.i] = list(toks)


class Ring:

    def __init__(self, bufs):
        self.bufs = bufs
        self.free = [[] for _ in bufs]
        self.held = [False for _ in bufs]
        self.i = 0

    def take(self):
        n = len(self.bufs)
        i = next(((self.i + j) % n for j in range(n) if not self.held[(self.i + j) % n]), self.i % n)
        self.i = i + 1
        assert not self.held[i], "slot taken before its readers are queued"
        self.held[i] = True
        return Slot(self, i)


def interleave(*gens):
    live = [[g, w, 0.0] for g, w in gens]
    while live:
        live.sort(key=lambda e: e[2])
        e = live[0]
        try:
            next(e[0])
            e[2] += e[1]
        except StopIteration:
            live.remove(e)


def build(nc, d, out):
    ctx = ExitStack()
    with ctx:
        def sem(name):
            return ctx.enter_context(nc.semaphore(name))

        PE, V, A, G, SP = (Queue(sem(n)) for n in ("s_pe", "s_dve", "s_act", "s_pool", "s_sp"))
        nvt, nvs = nc.vector.tensor_tensor, nc.vector.tensor_scalar
        stt = nc.vector.scalar_tensor_tensor
        act = nc.scalar.activation
        mmul = nc.tensor.matmul
        dsem = {}

        def dma(after, name, dst, src, q=None):
            if name not in dsem:
                dsem[name] = [sem(name), 0]
            q = q or SP
            return q.dma(after, dsem[name], (nc.scalar if q is A else nc.sync).dma_start, dst, src)

        def alloc(stack):
            def sb(name, shape, dt=F32):
                return stack.enter_context(nc.sbuf_tensor(name, shape, dt))
            return sb

        def group(after, mms):
            PE.wait(*after)
            for m in mms[:-1]:
                PE.quiet(mmul, m[0], m[1], m[2], start=m[3], stop=m[4], skip_group_check=True)
            m = mms[-1]
            return PE.do([], mmul, m[0], m[1], m[2], start=m[3], stop=m[4], skip_group_check=True)

        def transposes(after, pairs, ident):
            PE.wait(*after)
            for o, i in pairs[:-1]:
                PE.quiet(nc.tensor.transpose, o, i, ident)
            return PE.do([], nc.tensor.transpose, pairs[-1][0], pairs[-1][1], ident)

        def chain(o, ks):
            n = len(ks)
            return [(o, l, r, i == 0, i == n - 1) for i, (l, r) in enumerate(ks)]

        def barrier():
            toks = [q.last() for q in (PE, V, A, G)] + [(s[0], s[1]) for s in dsem.values() if s[1]]
            for q in (PE, V, A, G, SP):
                q.wait(*toks)

        sb = alloc(ctx)
        PS = [ctx.enter_context(nc.psum_tensor(f"ps{i}", [128, 512], F32)) for i in range(8)]
        xT = sb("xT", [128, 2, T])
        xn = sb("xn", [128, 2, T])
        ident = sb("ident", [128, 128])
        identb = sb("identb", [128, 128], BF16)
        onesm = sb("onesm", [128, 128])
        epsc = sb("epsc", [128, 1])
        onec = sb("onec", [128, 1])

        xload = [dma([], f"x{n}", xT[:, :, n * BW:(n + 1) * BW], d["x"][:, :, n * BW:(n + 1) * BW],
                     A if n % 2 else SP) for n in range(NB)]

        g1 = G.do([], nc.gpsimd.memset, ident[:, :], 0.0)
        g1 = G.do([g1], nc.gpsimd.affine_select, out=ident[:, :], in_=ident[:, :], compare_op=ALU.not_equal,
                  fill=1.0, base=0, pattern=[[-1, 128]], channel_multiplier=1)
        c_idb = V.do([g1], nc.vector.tensor_copy, identb[:, :], ident[:, :])
        V.do([], nc.vector.memset, onesm[:, :], 1.0 / 256.0)
        V.do([], nc.vector.memset, epsc[:, :], EPS)
        c_one = V.do([], nc.vector.memset, onec[:, :], 1.0)

        rstd = Ring([sb(f"rstd{i}", [128, 8]) for i in range(4)])
        xw = {n: None for n in range(NB)}

        def blk(t, k, n):
            return t[:, k, n * BW:(n + 1) * BW]

        def norm_stages(src, src_ready, dst, R, ring_t, psr, scale_bias=None, dst_free=()):
            p = psr.take()
            t1 = group([src_ready, p.free, c_one], chain(p.ap[:, :], [(onesm[:, :], src[:, k, :]) for k in range(2)]))
            xc = ring_t.take() if scale_bias is not None else None
            xa = xc.ap[:, :, :] if xc else dst
            v1 = V.do([t1, xc.free if xc else list(dst_free)], nvt, xa, src,
                      p.ap[:, None, :].broadcast_to([128, 2, BW]), ALU.subtract)
            p.release(v1)
            sq = ring_t.take()
            a1 = A.do([v1, sq.free], act, sq.ap[:, :, :], xa, ACT.Square)
            yield
            p = psr.take()
            mms = []
            for c in range(4):
                mms += chain(p.ap[:, c:c + 1], [(sq.ap[:, k, c * 128:(c + 1) * 128], onesm[:, 0:1])
                                                for k in range(2)])
            t2 = group([a1, p.free], mms)
            sq.release(t2)
            rs = rstd.take()
            a2 = A.do([t2, rs.free], act, rs.ap[:, 0:4], p.ap[:, 0:4], ACT.Sqrt, bias=epsc[:, 0:1])
            p.release(a2)
            v2 = V.do([a2], nc.vector.reciprocal, rs.ap[:, 4:8], rs.ap[:, 0:4])
            yield
            p = psr.take()
            v2 = group([v2, g1, p.free], [(p.ap[:, c * 128:(c + 1) * 128],
                                           rs.ap[:, 4 + c:5 + c].broadcast_to([128, 128]), ident[:, :], True, True)
                                          for c in range(4)])
            rs.release(v2)
            rb = p.ap[:, None, :].broadcast_to([128, 2, BW])
            if scale_bias is None:
                tok = V.do([v2], nvt, dst, dst, rb, ALU.mult)
                p.release(tok)
            else:
                s_, b_ = scale_bias
                own = dst is None
                dst = xc.ap if own else dst
                g_ = V.do([v2], nvt, xc.ap[:, :, :], xc.ap[:, :, :], rb, ALU.mult)
                p.release(g_)
                for k in range(2):
                    tok = V.do([g_, *dst_free], nvs, dst[:, k, :], xc.ap[:, k, :], s_[:, k:k + 1], b_[:, k:k + 1],
                               ALU.mult, ALU.add)
                if own:
                    R.append(xc)
                else:
                    xc.release(tok)
            R.append(tok)

        def layer_norm_all(src_ready, ring_t, psr, beside=None):
            beside = beside or iter(())
            toks = [[] for _ in range(NB)]
            gens = [norm_stages(xT[:, :, n * BW:(n + 1) * BW], src_ready[n], xn[:, :, n * BW:(n + 1) * BW],
                                toks[n], ring_t, psr) for n in range(NB)]
            for n in range(NB + 2):
                if n < NB:
                    next(gens[n])
                    next(beside, None)
                if 0 < n <= NB:
                    next(gens[n - 1])
                if n > 1:
                    for _ in gens[n - 2]:
                        pass
                    next(beside, None)
                    next(beside, None)
            for _ in beside:
                pass
            return [t[0] for t in toks]

        def xs(n, k):
            return blk(xn, k, n)

        def layer0(ready):
            ph = ExitStack()
            sb = alloc(ph)
            Wq, Wk = sb("Wq", [128, 2, 256]), sb("Wk", [128, 2, 256])
            Wv, Wg = sb("Wv", [128, 2, 512]), sb("Wg", [128, 2, 512])
            W1g = sb("Wgk1", [128, 2, 16])
            W2g_ = sb("Wgk2", [16, 256])
            W2g = W2g_[:, :]
            combT_ = sb("combT", [16, BW], F32R)
            combT = combT_[:, :]
            Wo = sb("Wo", [128, 4, 256])
            vec = sb("vec0", [128, 3])
            Wr = sb("Wr", [128, 2, 8])
            F1, F3 = sb("F1", [128, 8, 2, 384]), sb("F3", [128, 8, 2, 384])
            F2 = sb("F2", [128, 8, 3, 256])
            for t_, n_ in ((Wr, "Wr"), (W1g, "Wgk1"), (Wq, "Wq"), (Wk, "Wk"), (Wv, "Wv"), (Wg, "Wg"), (Wo, "Wo")):
                w_att = dma([], "w0", t_[:, :, :], d[n_])
            w_att = dma([], "w0", W2g, d["Wgk2"])
            w_att = dma([], "w0", vec[:, :], d["vec0"])
            w_ffn = []
            for e in range(8):
                for t_, n_ in ((F1, "F1"), (F3, "F3"), (F2, "F2")):
                    tok = dma([], f"w0f{e}", t_[:, e, :, :], d[n_][:, e, :, :])
                w_ffn.append(tok)
            psa = Ring(PS[0:3])
            psf = Ring(PS[3:6])
            pacc = Ring(PS[6:8])
            QK = sb("QK", [128, 4, BW])
            ob = sb("ob", [128, 4, BW])
            lnr = layer_norm_all(ready, Ring([t_[:, i:i + 2, :] for t_ in (QK, ob) for i in (0, 2)]), psf)
            hw = Ring([sb(f"hw{i}", [128, BW]) for i in range(4)])

            tri01 = sb("tri01", [128, 1, 128])
            g2 = G.do([], nc.gpsimd.memset, tri01[:, :, :], 1.0)
            c_tri = G.do([g2], nc.gpsimd.affine_select, out=tri01[:, :, :], in_=tri01[:, :, :],
                         compare_op=ALU.is_ge, fill=0.0, base=0, pattern=[[0, 1], [1, 128]], channel_multiplier=-1)
            resm = sb("resm", [128, 4, 128])
            c_res = G.do([], nc.gpsimd.memset, resm[:, :, :], 1.0)
            c_res = G.do([c_res], nc.gpsimd.memset, resm[:, :, 0:1], 0.0)
            S = sb("S", [128, 2, 128])
            Ss = sb("Ss", [128, 4, 128])
            z_ss = V.do([], nc.vector.memset, Ss[:, :, :], 0.0)
            U2 = sb("U2", [128, 2, 128])
            cum = sb("cum", [128, BW])
            D = sb("D", [128, BW])
            ex = Ring([sb(f"ex{i}", [128, BW]) for i in range(2)])
            qh, kh = [QK[:, i, :] for i in range(2)], [QK[:, 2 + i, :] for i in range(2)]
            ebm, ebe, eem = (sb(n_, [128, 2, 4]) for n_ in ("ebm", "ebe", "eem"))
            vr = Ring([sb(f"vt{i}", [128, 512]) for i in range(2)])
            at = sb("at", [128, 4, 128])
            kt = sb("kt", [128, 256])
            g16 = at[0:16, :, :].rearrange("p a b -> p (a b)")
            st = {"ob": [lnr[-1]], "qk": [lnr[-1]], "e": [], "S": None, "Ss": None, "g16": None,
                  "at": None, "kt": None, "U2": None, "cum": None, "D": None}
            done = []

            def attn():
                for n in range(NB):
                    lr = lnr[n]
                    p = psa.take()
                    t_ = group([lr, w_att, p.free], chain(p.ap[0:16, :], [(W1g[:, k, :], xs(n, k)) for k in range(2)]))
                    v_ = V.do([t_, st["g16"], st["at"]], nc.vector.tensor_copy, g16, p.ap[0:16, :])
                    p.release(v_)
                    for j in range(2):
                        yield
                        p = psa.take()
                        t_ = group([v_, p.free], [(p.ap[:, :], W2g[:, j * 128:(j + 1) * 128], g16, True, True)])
                        st["g16"] = t_
                        e1, e2 = ex.take(), ex.take()
                        a_ = A.do([t_, e1.free], act, e1.ap[:, :], p.ap[:, :], ACT.Abs, bias=vec[:, j:j + 1])
                        a_ = A.do([a_], act, e1.ap[:, :], e1.ap[:, :], ACT.Exp, scale=-1.0)
                        a_ = A.do([a_, c_one], act, e1.ap[:, :], e1.ap[:, :], ACT.Ln, bias=onec[:, 0:1])
                        m_ = V.do([t_, a_, e2.free], nvs, e2.ap[:, :], p.ap[:, :], vec[:, j:j + 1], 0.0, ALU.add,
                                  ALU.min)
                        p.release(m_)
                        m_ = V.do([m_, a_], nvt, e2.ap[:, :], e2.ap[:, :], e1.ap[:, :], ALU.subtract)
                        e1.release(m_)
                        c_ = V.do([m_, c_res, st["cum"]], nc.vector.tensor_tensor_scan, cum[:, :],
                                  resm[:, :, :].rearrange("p a b -> p (a b)"), e2.ap[:, :], 0.0, ALU.mult, ALU.add)
                        e2.release(c_)
                        cv = cum[:, :].rearrange("p (c t) -> p c t", c=4)
                        dv = D[:, :].rearrange("p (c t) -> p c t", c=4)
                        d_ = V.do([c_, st["D"]], nvt, dv, cv, cv[:, :, 63:64].broadcast_to([128, 4, 128]),
                                  ALU.subtract)
                        a1 = A.do([d_, *st["e"]], act, ebm[:, j, :], cv[:, :, 63], ACT.Exp, scale=1 / 16)
                        a1 = A.do([], act, ebe[:, j, :], cv[:, :, 127], ACT.Exp, scale=1 / 16)
                        a1 = A.do([], act, eem[:, j, :], dv[:, :, 127], ACT.Exp, scale=1 / 16)
                        st["cum"] = a1
                        e1, e2 = ex.take(), ex.take()
                        aq = A.do([d_, e1.free], act, e1.ap[:, :], D[:, :], ACT.Exp, scale=1 / 16)
                        ak = A.do([e2.free], act, e2.ap[:, :], D[:, :], ACT.Exp, scale=-1 / 16)
                        st["D"] = ak
                        yield
                        for w_, o_, e_, sc_, a_ in ((Wq, qh, e1, 0.125, aq), (Wk, kh, e2, 1.0, ak)):
                            p = psa.take()
                            t_ = group([p.free], chain(p.ap[:, :], [(w_[:, k, j * 128:(j + 1) * 128], xs(n, k))
                                                                    for k in range(2)]))
                            s_ = V.do([t_, a_, *st["qk"]], stt, out=o_[j], in0=p.ap[:, :], scalar=sc_,
                                      in1=e_.ap[:, :], op0=ALU.mult, op1=ALU.mult)
                            e_.release(s_)
                            p.release(s_)
                    qk_ready = s_
                    e_ready = a1
                    if n % 4 == 0:
                        st["S"] = V.do([st["S"], st["Ss"]], nc.vector.memset, S[:, :, :], 0.0)
                    for c in range(4):
                        cs = slice(c * 128, (c + 1) * 128)
                        yield
                        p = psa.take()
                        t_ = group([p.free], chain(p.ap[:, :], [
                            (xn[:, k, n * BW + c * 128:n * BW + (c + 1) * 128], Wv[:, k, :]) for k in range(2)]))
                        vs = vr.take()
                        vt = vs.ap
                        vtk = A.do([t_, vs.free], act, vt[:, :], p.ap[:, :], ACT.Copy)
                        p.release(vtk)
                        for h in range(4):
                            hs = slice(64 * (h % 2), 64 * (h % 2) + 64)
                            ss = V.do([st["S"], st["Ss"], e_ready, z_ss], nvs, Ss[hs, h, :], S[hs, h // 2, :],
                                      ebm[hs, h // 2, c:c + 1], None, ALU.mult)
                        yield
                        p = psa.take()
                        t_ = transposes([qk_ready, g1, p.free], [(p.ap[:, j * 128:(j + 1) * 128], kh[j][:, cs])
                                                                  for j in range(2)], ident[:, :])
                        ktk = V.do([t_, st["kt"]], nc.vector.tensor_copy, kt[:, :], p.ap[:, 0:256])
                        p.release(ktk)
                        pp = [psa.take(), psa.take()]
                        mms = []
                        for h in (0, 2, 1, 3):
                            hs = slice(64 * (h % 2), 64 * (h % 2) + 64)
                            mms.append((pp[h % 2].ap[:, (h // 2) * 128:(h // 2 + 1) * 128], kh[h // 2][hs, cs],
                                        qh[h // 2][hs, cs], True, True))
                        t_ = group([pp[0].free, pp[1].free], mms)
                        for hh in range(2):
                            att = V.do([t_, c_tri, st["at"], st["g16"]], nvt, at[:, hh:4:2, :],
                                       pp[hh].ap[:, 0:256].rearrange("p (h t) -> p h t", h=2),
                                       tri01[:, :, :].broadcast_to([128, 2, 128]), ALU.mult)
                            pp[hh].release(att)
                        yield
                        p = psa.take()
                        mms = []
                        for h in range(4):
                            o_ = p.ap[:, h * 128:(h + 1) * 128]
                            mms.append((o_, vt[:, h * 128:(h + 1) * 128], at[:, h, :], True, False))
                            mms.append((o_, Ss[:, h, :], qh[h // 2][:, cs], False, True))
                        to = group([att, ss, vtk, p.free], mms)
                        st["at"] = st["Ss"] = to
                        obt = A.do([to, *st["ob"]], act, ob[:, :, cs],
                                   p.ap[:, :].rearrange("p (h t) -> p h t", h=4), ACT.Copy)
                        p.release(obt)
                        p = psa.take()
                        tu = group([ktk, p.free], [(p.ap[:, j * 256:(j + 1) * 256], kt[:, j * 128:(j + 1) * 128],
                                                    vt[:, j * 256:(j + 1) * 256], True, True) for j in range(2)])
                        st["kt"] = tu
                        vs.release(tu)
                        for j in range(2):
                            for h in range(2):
                                hs = slice(64 * h, 64 * h + 64)
                                u_ = V.do([tu, st["U2"], e_ready], nvs, U2[hs, j, :],
                                          p.ap[hs, j * 256 + h * 128:j * 256 + (h + 1) * 128], eem[hs, j, c:c + 1],
                                          None, ALU.mult)
                        p.release(u_)
                        for j in range(2):
                            s_ = V.do([u_, ss], stt, out=S[:, j, :], in0=S[:, j, :], scalar=ebe[:, j, c:c + 1],
                                      in1=U2[:, j, :], op0=ALU.mult, op1=ALU.add)
                        st["U2"] = st["S"] = s_
                    st["qk"], st["e"] = [tu, to], [s_]
                    yield
                    pr = []
                    for h in range(4):
                        e1 = ex.take()
                        a_ = A.do([obt, e1.free], act, e1.ap[:, :], ob[:, h, :], ACT.Square)
                        p = psa.take()
                        t_ = group([a_, p.free], [(p.ap[:, :], onesm[:, :], e1.ap[:, :], True, True)])
                        a_ = A.do([t_], act, e1.ap[:, :], p.ap[:, :], ACT.Sqrt, bias=epsc[:, 0:1], scale=2.0)
                        p.release(a_)
                        v_ = V.do([a_], nc.vector.reciprocal, e1.ap[:, :], e1.ap[:, :])
                        v_ = V.do([v_], stt, out=ob[:, h, :], in0=ob[:, h, :], scalar=vec[:, 2:3],
                                  in1=e1.ap[:, :], op0=ALU.mult, op1=ALU.mult)
                        e1.release(v_)
                        p = psa.take()
                        t_ = group([p.free], chain(p.ap[:, :], [(Wg[:, k, h * 128:(h + 1) * 128], xs(n, k))
                                                                for k in range(2)]))
                        e1 = ex.take()
                        a_ = A.do([t_, e1.free], act, e1.ap[:, :], p.ap[:, :], ACT.Silu)
                        p.release(a_)
                        pr.append(G.do([v_, a_], nc.gpsimd.tensor_tensor, ob[:, h, :], ob[:, h, :], e1.ap[:, :],
                                       ALU.mult))
                        e1.release(pr[-1])
                        yield
                    for m in range(2):
                        p = psa.take()
                        t_ = group([pr[-1], p.free], chain(p.ap[:, :], [(Wo[:, h, m * 128:(m + 1) * 128], ob[:, h, :])
                                                                        for h in range(4)]))
                        v_ = xw[n] = V.do([t_, xw[n]], nvt, blk(xT, m, n), blk(xT, m, n), p.ap[:, :], ALU.add)
                        p.release(v_)
                    st["ob"] = [t_]
                    done.append(v_)
                    yield

            iot = sb("iot", [128, 8])
            ioti = sb("ioti", [128, 8], I32)
            c_io = G.do([], nc.gpsimd.iota, ioti[:, :], pattern=[[1, 8]], base=0, channel_multiplier=0)
            c_io = V.do([c_io], nc.vector.tensor_copy, iot[:, :], ioti[:, :])
            lg = sb("lg", [128, 4, 8])
            m8 = sb("m8", [128, 4, 8])
            ix = sb("ix", [128, 4, 8], U32)
            ixf = sb("ixf", [128, 4, 8])
            w8 = sb("w8", [128, 4, 4])
            cb1 = sb("cb1", [128, 4, 8])
            cb2 = sb("cb2", [128, 4, 8])
            cba = sb("cba", [128, 4, 8], F32R)
            cbp = sb("cbp", [128, 4, 16])
            sel = sb("sel", [16, 8], F32R)
            c_sel = V.do([g1], nvt, sel[:, :], ident[0:16, 0:8], ident[0:16, 8:16], ALU.add)
            cbs = Ring([sb(f"cbs{i}", [128, BW]) for i in range(2)])
            cfree = []
            fdone = []

            def gate_weights(n):
                p = psf.take()
                mms = []
                for c in range(4):
                    mms += chain(p.ap[:, c * 8:(c + 1) * 8], [
                        (xn[:, k, n * BW + c * 128:n * BW + (c + 1) * 128], Wr[:, k, :]) for k in range(2)])
                t_ = group([lnr[n], w_att, p.free], mms)
                v_ = V.do([t_, V.last()], nc.vector.tensor_copy, lg[:, :, :].rearrange("p a b -> p (a b)"),
                          p.ap[:, 0:32])
                p.release(v_)
                for c in range(4):
                    v1 = V.do([v_], nc.vector.max, m8[:, c, :], lg[:, c, :])
                for c in range(4):
                    v2 = V.do([v1], nc.vector.max_index, ix[:, c, :], m8[:, c, :], lg[:, c, :])
                v2 = V.do([v2], nc.vector.tensor_copy, ixf[:, :, :], ix[:, :, :])
                v3 = V.do([v1], nvt, w8[:, :, 0:1], m8[:, :, 1:2], m8[:, :, 0:1], ALU.subtract)
                a_ = A.do([v3], act, w8[:, :, 1:2], w8[:, :, 0:1], ACT.Exp)
                v3 = V.do([a_], nvs, w8[:, :, 2:3], w8[:, :, 1:2], 1.0, None, ALU.add)
                v3 = V.do([v3], nc.vector.reciprocal, w8[:, :, 2:3], w8[:, :, 2:3])
                v3 = V.do([v3, v2], nvt, w8[:, :, 3:4], w8[:, :, 1:2], w8[:, :, 2:3], ALU.mult)
                for c in range(4):
                    V.do([v3, c_io], nvs, cb1[:, c, :], iot[:, :], ixf[:, c, 0:1], w8[:, c, 2:3], ALU.is_equal,
                         ALU.mult)
                    v4 = V.do([v3, c_io], nvs, cb2[:, c, :], iot[:, :], ixf[:, c, 1:2], w8[:, c, 3:4],
                              ALU.is_equal, ALU.mult)
                v4 = V.do([v4], nvt, cb1[:, :, :], cb1[:, :, :], cb2[:, :, :], ALU.add)
                v4 = V.do([v4], nc.vector.tensor_copy, cba[:, :, :], cb1[:, :, :])
                V.do([v4], nc.vector.tensor_copy, cbp[:, :, 0:8], cba[:, :, :].bitcast(F32))
                v4 = V.do([v4], nvt, cbp[:, :, 8:16], cb1[:, :, :], cba[:, :, :].bitcast(F32), ALU.subtract)
                yield
                p = psf.take()
                t_ = transposes([v4, g1, p.free], [(p.ap[0:16, c * 128:(c + 1) * 128], cbp[:, c, :])
                                                   for c in range(4)], ident[:, :])
                v_ = V.do([t_, *cfree], nc.vector.tensor_copy, combT, p.ap[0:16, :])
                p.release(v_)
                return v_

            def ffn():
                cr = yield from gate_weights(0)
                for n in range(NB):
                    acc = [pacc.take(), pacc.take()]
                    pend = None
                    for e in range(8):
                        p = psf.take()
                        t_ = group([cr, c_sel, p.free], [(p.ap[:, :], sel[:, e:e + 1].broadcast_to([16, 128]), combT,
                                                   True, True)])
                        cb = cbs.take()
                        cbt = A.do([t_, cb.free], act, cb.ap[:, :], p.ap[:, :], ACT.Copy)
                        p.release(cbt)
                        for m in range(3):
                            ms = slice(m * 128, (m + 1) * 128)
                            ph_, pg_ = psf.take(), psf.take()
                            th = group([w_ffn[e], ph_.free], chain(ph_.ap[:, :], [(F1[:, e, k, ms], xs(n, k))
                                                                                  for k in range(2)]))
                            s_ = hw.take()
                            a_ = A.do([th, s_.free], act, s_.ap[:, :], ph_.ap[:, :], ACT.Silu)
                            ph_.release(a_)
                            tg = group([pg_.free], chain(pg_.ap[:, :], [(F3[:, e, k, ms], xs(n, k))
                                                                        for k in range(2)]))
                            v_ = V.do([tg, a_], nvt, s_.ap[:, :], s_.ap[:, :], pg_.ap[:, :], ALU.mult)
                            pg_.release(v_)
                            g_ = G.do([v_, cbt], nc.gpsimd.tensor_tensor, s_.ap[:, :], s_.ap[:, :], cb.ap[:, :],
                                      ALU.mult)
                            if m == 2:
                                cb.release(g_)
                            yield
                            if pend is not None:
                                down(acc, *pend)
                            pend = (s_, g_, e, m)
                    cfree[:] = [t_]
                    if n + 1 < NB:
                        cr = yield from gate_weights(n + 1)
                    ta = down(acc, *pend)
                    for m in range(2):
                        v_ = xw[n] = V.do([ta, xw[n]], nvt, blk(xT, m, n), blk(xT, m, n), acc[m].ap[:, :], ALU.add)
                        acc[m].release(v_)
                    fdone.append(v_)

            def down(acc, s_, g_, e, m):
                mms = [(acc[o].ap[:, :], F2[:, e, m, o * 128:(o + 1) * 128], s_.ap[:, :], e == 0 and m == 0,
                        e == 7 and m == 2) for o in range(2)]
                ta = group([g_] + (acc[0].free + acc[1].free if e == 0 and m == 0 else []), mms)
                s_.release(ta)
                return ta

            interleave((attn(), 1.15), (ffn(), 1.0))
            barrier()
            ph.close()
            return [[done[n], fdone[n]] for n in range(NB)]

        def layer1(ready):
            ph = ExitStack()
            sb = alloc(ph)
            GA, GB = sb("gathA", [128, 8, 768]), sb("gathB", [128, 8, 768])
            Wi = sb("mWi", [128, 2, 1024])
            Wd = sb("mWd", [128, 4, 512])
            Wu = sb("mWo", [128, 4, 256])
            Bm = sb("mB", [128, 4, 16])
            Cm = sb("mC", [16, 512])
            Al = sb("mA", [16, 1])
            vec = sb("vec1", [128, 32])
            cw = sb("mcw", [128, 4, 4])
            Pi = sb("pWi", [128, 2, 512])
            Po = sb("pWo", [128, 4, 256])
            WS = sb("WS", [128, 2, 2048])
            gflat = GA[:, :, :].rearrange("p a b -> p (a b)")
            WqK = gflat[:, 0:4096].rearrange("p (a b) -> p a b", a=16)
            keys = gflat[:, 4096:6144].rearrange("p (a b) -> p a b", a=16)
            w_k = dma([], "w1k", WqK, d["pWq"])
            w_k = dma([], "w1k", keys, d["keys"])
            for t_, n_ in ((Wi, "mWi"), (Wd, "mWd"), (Wu, "mWo"), (Bm, "mB"), (cw, "mcw")):
                w_m = dma([], "w1m", t_[:, :, :], d[n_])
            for t_, n_ in ((Cm, "mC"), (Al, "mA"), (vec, "vec1")):
                w_m = dma([], "w1m", t_[:, :], d[n_])
            for t_, n_ in ((Pi, "pWi"), (Po, "pWo")):
                w_p = dma([], "w1p", t_[:, :, :], d[n_])
            gam, bet, cvb, bd, Dv = vec[:, 0:2], vec[:, 2:4], vec[:, 4:8], vec[:, 8:12], vec[:, 12:16]
            psm = Ring(PS[0:3])
            psk = Ring(PS[3:8])
            xsb = sb("xsb", [128, 4, 3 + BW])
            u = sb("u", [128, 4, BW])
            big = Ring([sb(f"bg{i}", [128, 2, BW]) for i in range(2)])
            wst = []

            def score_weights():
                for _ in range(10):
                    yield
                for kk in range(2):
                    for g in range(4):
                        p = psk.take()
                        t_ = group([w_k, p.free], [(p.ap[:, i * 128:(i + 1) * 128],
                                                    WqK[:, 4 * g + i, kk * 128:(kk + 1) * 128], keys[:, 4 * g + i, :],
                                                    True, True) for i in range(4)])
                        wst.append(A.do([t_], act, WS[:, kk, g * 512:(g + 1) * 512], p.ap[:, :], ACT.Copy))
                        p.release(wst[-1])
                        yield

            lnr = layer_norm_all(ready, Ring([b_ for b_ in big.bufs] + [u[:, 0:2, :], u[:, 2:4, :]]), psm,
                                 score_weights())
            big.free = [[lnr[-1]], [lnr[-1]]]
            ws_used = PE.last()
            sA = sb("sA", [16, 1])
            a_ = A.do([w_m], act, sA[:, :], Al[:, :], ACT.Exp)
            c_A = A.do([a_], act, sA[:, :], sA[:, :], ACT.Copy, scale=-1.0)
            o16 = sb("o16", [128, 16])
            c_o16 = V.do([], nc.vector.memset, o16[:, :], 1.0 / 512.0)
            tmp = Ring([sb(f"tm{i}", [128, BW]) for i in range(4)])
            dl = sb("dl", [16, BW])
            Bx = hs = sb("Bx", [16, BW])
            done, fdone = [], []

            def mamba():
                s = {"xsb": [], "u": [lnr[-1]], "dl": [], "Bx": [], "halo": None}
                for n in range(NB):
                    R = []
                    yield from norm_stages(xn[:, :, n * BW:(n + 1) * BW], lnr[n], None, R, big, psm,
                                           (gam, bet), dst_free=[w_m])
                    hslot, hr = R
                    hn = hslot.ap
                    yield
                    if n % 4 == 0:
                        hal = V.do([*s["xsb"]], nc.vector.memset, xsb[:, :, 0:3], 0.0)
                    else:
                        hal = V.do([*s["xsb"]], nc.vector.tensor_copy, xsb[:, :, 0:3], xsb[:, :, BW:BW + 3])
                    ur = []
                    for i in range(4):
                        p = psm.take()
                        t_ = group([hr, p.free], chain(p.ap[:, :], [(Wi[:, k, i * 128:(i + 1) * 128], hn[:, k, :])
                                                                    for k in range(2)]))
                        a_ = A.do([t_, hal], act, xsb[:, i, 3:3 + BW], p.ap[:, :], ACT.Copy)
                        p.release(a_)
                        c1 = tmp.take()
                        v_ = V.do([a_, c1.free], nvs, c1.ap[:, :], xsb[:, i, 0:BW], cw[:, i, 0:1], None, ALU.mult)
                        for k in range(1, 4):
                            v_ = V.do([v_], stt, out=c1.ap[:, :], in0=xsb[:, i, k:k + BW], scalar=cw[:, i, k:k + 1],
                                      in1=c1.ap[:, :], op0=ALU.mult, op1=ALU.add)
                        ur.append(A.do([v_, *s["u"]], act, u[:, i, :], c1.ap[:, :], ACT.Silu, bias=cvb[:, i:i + 1]))
                        c1.release(ur[-1])
                        yield
                    s["xsb"] = [v_]
                    pb = psm.take()
                    tb = group([ur[3], pb.free], chain(pb.ap[0:16, :], [(Bm[:, k, :], u[:, k, :]) for k in range(4)]))
                    bxa = A.do([tb, *s["Bx"]], act, Bx[:, :], pb.ap[0:16, :], ACT.Copy)
                    pb.release(bxa)
                    sp = []
                    for i in range(4):
                        p = psm.take()
                        t_ = group([p.free], chain(p.ap[:, :], [(Wd[:, k, i * 128:(i + 1) * 128], u[:, k, :])
                                                                for k in range(4)]))
                        e1, e2 = tmp.take(), tmp.take()
                        rl = e2.ap[:, :]
                        a_ = A.do([t_, e1.free], act, e1.ap[:, :], p.ap[:, :], ACT.Abs, bias=bd[:, i:i + 1])
                        v_ = V.do([a_, e2.free], nvs, rl, p.ap[:, :], bd[:, i:i + 1], 0.0, ALU.add, ALU.max)
                        p.release(v_)
                        a_ = A.do([a_], act, e1.ap[:, :], e1.ap[:, :], ACT.Exp, scale=-1.0)
                        yield
                        if i == 0:
                            pd = psm.take()
                            pe1 = e1
                            pv_ = V.do([a_], nvs, e1.ap[:, :], e1.ap[:, :], 1.0, None, ALU.add)
                        else:
                            pv_ = V.do([a_, pv_], stt, out=pe1.ap[:, :], in0=e1.ap[:, :], scalar=1.0,
                                       in1=pe1.ap[:, :], op0=ALU.add, op1=ALU.mult)
                            e1.release(pv_)
                        td = group([v_, c_o16, pd.free], [(pd.ap[0:16, :], o16[:, :], rl, i == 0, False)])
                        e2.release(td)
                    a_ = A.do([pv_], act, pe1.ap[:, :], pe1.ap[:, :], ACT.Ln)
                    yield
                    td = group([a_], [(pd.ap[0:16, :], o16[:, :], pe1.ap[:, :], False, True)])
                    pe1.release(td)
                    v_ = V.do([td, *s["dl"]], nc.vector.tensor_copy, dl[:, :], pd.ap[0:16, :])
                    pd.release(v_)
                    v_ = V.do([v_, bxa], nvt, Bx[:, :], Bx[:, :], dl[:, :], ALU.mult)
                    a_ = A.do([v_, c_A], act, dl[:, :], dl[:, :], ACT.Exp, scale=sA[:, 0:1])
                    init = 0.0 if n % 4 == 0 else hl[:, 0:1]
                    v_ = V.do([v_, a_, s["halo"]], nc.vector.tensor_tensor_scan, hs[:, :], dl[:, :],
                              Bx[:, :], init, ALU.mult, ALU.add)
                    s["dl"] = [v_]
                    s["halo"] = V.do([v_], nc.vector.tensor_copy, hl[:, 0:1], hs[:, BW - 1:BW])
                    yield
                    for i in range(4):
                        p = psm.take()
                        t_ = group([v_, p.free], [(p.ap[:, :], Cm[:, i * 128:(i + 1) * 128], hs[:, :], True, True)])
                        y_ = V.do([t_, ur[i]], stt, out=u[:, i, :], in0=u[:, i, :], scalar=Dv[:, i:i + 1],
                                  in1=p.ap[:, :], op0=ALU.mult, op1=ALU.add)
                        p.release(y_)
                        p = psm.take()
                        t_ = group([p.free], chain(p.ap[:, :], [(Wi[:, k, 512 + i * 128:512 + (i + 1) * 128],
                                                                 hn[:, k, :]) for k in range(2)]))
                        e1 = tmp.take()
                        gt = A.do([t_, e1.free], act, e1.ap[:, :], p.ap[:, :], ACT.Silu)
                        p.release(gt)
                        y_ = V.do([y_, gt], nvt, u[:, i, :], u[:, i, :], e1.ap[:, :], ALU.mult)
                        e1.release(y_)
                        yield
                    s["Bx"] = [t_, s["halo"]]
                    hslot.release(t_)
                    for m in range(2):
                        p = psm.take()
                        t_ = group([y_, p.free], chain(p.ap[:, :], [(Wu[:, k, m * 128:(m + 1) * 128], u[:, k, :])
                                                                    for k in range(4)]))
                        v_ = xw[n] = V.do([t_, xw[n]], nvt, blk(xT, m, n), blk(xT, m, n), p.ap[:, :], ALU.add)
                        p.release(v_)
                        v_ = xw[n] = V.do([v_], nvt, blk(xT, m, n), blk(xT, m, n), blk(xn, m, n), ALU.add)
                    s["u"] = [t_]
                    done.append(v_)
                    yield

            hl = sb("hl", [16, 1])
            mx = sb("mx", [128, 16, 8])
            mi = sb("mi", [128, 16, 8], U32)
            mif = sb("mif", [128, 16])
            idx = Ring([sb(f"idx{i}", [128, 8], U32) for i in range(3)])
            gte = Ring([sb(f"gte{i}", [128, 8]) for i in range(3)])
            gf = sb("gf", [128, 16])
            xt_ = sb("xt_", [128, 256])
            lin = sb("lin", [128, 16])
            hacc = sb("hacc", [128, 512])
            hg = sb("hg", [128, 512])
            jk = sb("jk", [128, 512])
            oacc = sb("oacc", [128, 256])
            hgT = sb("hgT", [128, 512])
            NT = 32

            def route(t, q):
                ts = slice(t * 128, (t + 1) * 128)
                for g in range(4):
                    p = psk.take()
                    tk = group([lnr[t // 4], wst[g], wst[4 + g], p.free], chain(p.ap[:, :], [
                        (xn[:, k, ts], WS[:, k, g * 512:(g + 1) * 512]) for k in range(2)]))
                    for i in range(4):
                        v1 = V.do([tk, q["mx"]], nc.vector.max, mx[:, 4 * g + i, :], p.ap[:, i * 128:(i + 1) * 128])
                    for i in range(4):
                        v2 = V.do([v1], nc.vector.max_index, mi[:, 4 * g + i, :], mx[:, 4 * g + i, :],
                                  p.ap[:, i * 128:(i + 1) * 128])
                    p.release(v2)
                    yield
                v3 = V.do([v2, q["mif"]], nc.vector.tensor_copy, mif[:, :], mi[:, :, 0])
                v4 = V.do([v3], stt, out=gf[:, 0:8], in0=mif[:, 0:8], scalar=128.0, in1=mif[:, 8:16], op0=ALU.mult,
                          op1=ALU.add)
                id_, gt_ = idx.take(), gte.take()
                v5 = V.do([v4, id_.free], nvs, id_.ap[:, :], gf[:, 0:8], 4095.0, None, ALU.min)
                q["mif"] = v5
                v6 = V.do([v1, gt_.free], nvt, gt_.ap[:, :], mx[:, 0:8, 0], mx[:, 8:16, 0], ALU.add)
                v6 = V.do([v6], nvs, gt_.ap[:, :], gt_.ap[:, :], 0.0, None, ALU.max)
                q["mx"] = v6
                q["out"] = (id_, gt_, v5, v6)

            def gather(half, buf, id_, v5, gfree):
                toks = []
                for h in range(8):
                    nm = f"g{half}{h}"
                    if nm not in dsem:
                        dsem[nm] = [sem(nm), 0]
                    toks.append(G.dma([v5, gfree[h]], dsem[nm], nc.gpsimd.indirect_dma_start, out=buf[:, h, :],
                                      out_offset=None, in_=d[f"tab{half}"],
                                      in_offset=bass.IndirectOffsetOnAxis(ap=id_.ap[:, h:h + 1], axis=0),
                                      bounds_check=4095, oob_is_err=False))
                return toks

            def peer():
                q = {"mx": None, "mif": None}
                last = {"hg": None, "x": None, "hT": None}
                rt = {}
                for t in range(2):
                    yield from route(t, q)
                    rt[t] = q["out"]
                ka = gather(0, GA, rt[0][0], rt[0][2], [ws_used] * 8)
                kb = gather(1, GB, rt[0][0], rt[0][2], [None] * 8)
                rt[0][0].release(*ka, *kb)

                def first_half(t):
                    ts = slice(t * 128, (t + 1) * 128)
                    p = psk.take()
                    t_ = transposes([g1, p.free], [(p.ap[:, k * 128:(k + 1) * 128], xn[:, k, ts]) for k in range(2)],
                                    ident[:, :])
                    xa = A.do([t_, last["x"]], act, xt_[:, :], p.ap[:, 0:256], ACT.Copy)
                    p.release(xa)
                    ph_ = psk.take()
                    th = group([w_p, ph_.free], chain(ph_.ap[:, :], [(xn[:, k, ts], Pi[:, k, :]) for k in range(2)]))
                    return xa, ph_, th

                def finish(t, hT, dg):
                    ts = slice(t * 128, (t + 1) * 128)
                    p = psk.take()
                    mms = []
                    for m in range(2):
                        ms = slice(m * 128, (m + 1) * 128)
                        mms += chain(p.ap[:, ms], [(Po[:, k, ms], hgT[:, k * 128:(k + 1) * 128]) for k in range(4)]
                                     + [(oacc[:, ms], ident[:, :])])
                    t_ = group([hT, dg, p.free], mms)
                    last["hT"] = last["o"] = t_
                    v_ = xw[t // 4] = V.do([t_, xw[t // 4]], nvt, xT[:, :, ts], xT[:, :, ts], p.ap[:, 0:256].rearrange("p (m t) -> p m t", m=2),
                              ALU.add)
                    p.release(v_)
                    fdone.append(v_)

                last["o"] = last["fh"] = None
                junk = [[hacc, None], [jk, None]]
                fh = first_half(0)
                fin = None
                for t in range(NT):
                    gt_, v6 = rt[t][1], rt[t][3]
                    xa, ph_, th = fh
                    for h in range(8):
                        jt = junk[h % 2]
                        v_ = jt[1] = V.do([xa, ka[h], jt[1], last["fh"]], nc.vector.tensor_tensor_reduce,
                                          out=jt[0][:, 0:256], in0=xt_[:, :], in1=GA[:, h, 0:256], scale=1.0,
                                          scalar=0.0, op0=ALU.mult, op1=ALU.add, accum_out=lin[:, h:h + 1])
                        if h == 3:
                            yield
                    last["x"] = v_
                    yield
                    v_ = V.do([v_, v6], nvt, lin[:, 0:8], lin[:, 0:8], gt_.ap[:, :], ALU.mult)
                    src = ph_.ap[:, :]
                    used = []
                    for h in range(8):
                        v_ = V.do([v_, th], stt, out=hacc[:, :], in0=GA[:, h, 256:768], scalar=lin[:, h:h + 1],
                                  in1=src, op0=ALU.mult, op1=ALU.add)
                        src = hacc[:, :]
                        used.append(v_)
                        if h == 0:
                            ph_.release(v_)
                        if h % 2:
                            yield
                    if t + 1 < NT:
                        ka = gather(0, GA, rt[t + 1][0], rt[t + 1][2], used)
                    a_ = A.do([v_, last["hg"]], act, hg[:, :], hacc[:, :], ACT.Gelu)
                    yield
                    rg = route(t + 2, q) if t + 2 < NT else iter(range(4))
                    for i, _ in enumerate(rg):
                        yield
                        if i == 1 and fin is not None:
                            finish(*fin)
                            yield
                    if t + 2 < NT:
                        rt[t + 2] = q["out"]
                    p = psk.take()
                    t_ = transposes([a_, p.free], [(p.ap[:, k * 128:(k + 1) * 128], hg[:, k * 128:(k + 1) * 128])
                                                   for k in range(4)], ident[:, :])
                    hT = A.do([t_, last["hT"]], act, hgT[:, :], p.ap[:, :], ACT.Copy)
                    p.release(hT)
                    for h in range(8):
                        jt = junk[h % 2]
                        v_ = jt[1] = V.do([a_, kb[h], jt[1]], nc.vector.tensor_tensor_reduce, out=jt[0][:, :],
                                          in0=hg[:, :], in1=GB[:, h, 0:512], scale=1.0, scalar=0.0, op0=ALU.mult,
                                          op1=ALU.add, accum_out=lin[:, 8 + h:9 + h])
                        if h % 2:
                            yield
                    last["hg"] = v_
                    v_ = last["fh"] = V.do([v_], nvt, lin[:, 8:16], lin[:, 8:16], gt_.ap[:, :], ALU.mult)
                    gt_.release(v_)
                    v_ = V.do([v_, last["o"]], nvs, oacc[:, :], GB[:, 0, 512:768], lin[:, 8:9], None, ALU.mult)
                    used = [v_]
                    for h in range(1, 8):
                        v_ = V.do([v_], stt, out=oacc[:, :], in0=GB[:, h, 512:768], scalar=lin[:, 8 + h:9 + h],
                                  in1=oacc[:, :], op0=ALU.mult, op1=ALU.add)
                        used.append(v_)
                        if h % 3 == 2:
                            yield
                    fin = (t, hT, v_)
                    if t + 1 < NT:
                        kb = gather(1, GB, rt[t + 1][0], rt[t + 1][2], used)
                        rt[t + 1][0].release(*ka, *kb)
                        fh = first_half(t + 1)
                    yield
                finish(*fin)

            interleave((mamba(), 4.2), (peer(), 1.0))
            barrier()
            ph.close()
            return [[done[n], fdone[4 * n + 3]] for n in range(NB)]

        def layer2(ready):
            ph = ExitStack()
            sb = alloc(ph)
            Wr = sb("rW", [128, 2, 256])
            W1 = sb("rW1", [128, 2, 1024])
            W2 = sb("rW2", [128, 8, 256])
            vec = sb("vec2", [128, 32])
            eh = sb("reh", [128, 4, BW])
            raw = eh[:, :, :].rearrange("p a b -> p (a b)").bitcast(U8).rearrange("p (a b) -> p a b", a=8)
            wr0 = dma([], "w2k0", raw[:, 0:4, :], d["k0"])
            for t_, n_ in ((Wr, "rWr"), (W1, "rW1"), (W2, "rW2")):
                w_r = dma([], "w2r", t_[:, :, :], d[n_])
            w_r = dma([], "w2r", vec[:, :], d["vec2"])
            K0, K1, K2 = (sb(n_, sh_, F32R) for n_, sh_ in (("K0", [128, 2, 1024]), ("K1", [128, 8, 1024]),
                                                           ("K2", [128, 8, 256])))
            e_, h_ = eh[:, 0:2, :], eh[:, 2:4, :]
            b_r, l1s, l1b, l2s, l2b = (vec[:, 2 * i:2 * i + 2] for i in range(5))
            b1, b2, sc = vec[:, 10:18], vec[:, 18:20], vec[:, 20:23]
            psr = Ring(PS[0:2])
            psb = Ring(PS[2:4])
            racc = Ring(PS[4:6])
            bacc_ = Ring(PS[6:8])
            big = Ring([sb(f"bh{i}", [128, 2, BW]) for i in range(2)])
            fa = sb("fa", [128, 5, BW])
            ft = Ring([fa[:, i, :] for i in range(3)])
            ac = Ring([fa[:, i, :] for i in (3, 4)])
            w_k = {}

            def signs():
                f_, u_ = fa[:, 4, :], None
                for _ in range(2):
                    yield
                for k in range(2):
                    for hf in range(2):
                        cs = slice(hf * 512, (hf + 1) * 512)
                        g_ = V.do([wr0, u_], nvs, f_, raw[:, 2 + k, cs], 2.0, None, ALU.mult)
                        u_ = V.do([g_], stt, out=K0[:, k, cs], in0=raw[:, k, cs], scalar=2.0, in1=f_, op0=ALU.mult,
                                  op1=ALU.subtract)
                        yield
                w_k[0] = u_
                wr = dma([u_], "w2k1", raw[:, :, :], d["k1"])
                for _ in range(3):
                    yield
                for k in range(8):
                    w_k[1] = V.do([wr], nvs, K1[:, k, :], raw[:, k, :], 2.0, -1.0, ALU.mult, ALU.add)
                    if k % 2:
                        yield
                wr = dma([w_k[1]], "w2k2", raw[:, 0:2, :].rearrange("p a b -> p (a b)"), d["k2"])
                for _ in range(3):
                    yield
                w_k[2] = V.do([wr], nvs, K2[:, :, :], raw[:, 0:2, :].rearrange("p a (b c) -> p (a b) c", b=4), 2.0,
                              -1.0, ALU.mult, ALU.add)

            lnr = layer_norm_all(ready, Ring(big.bufs + [fa[:, 0:2, :], fa[:, 2:4, :]]), psr, signs())
            w_k0, w_k1, w_k2 = (w_k[i] for i in range(3))
            for ring in (big, ft, ac):
                ring.free = [[lnr[-1], w_k0] for _ in ring.bufs]
            s2 = sb("s2c", [128, 2])
            c_s2 = V.do([w_r], nvs, s2[:, :], sc[:, 0:2], 2.0, None, ALU.mult)
            half = sb("half", [128, 1])
            c_half = V.do([], nc.vector.memset, half[:, :], 0.5)
            sig = [e_[:, i, :] for i in range(2)]
            rl = sb("rl", [128, 2])
            done, fdone = [], []

            def reten():
                s = {"rl": None, "e": w_k2, "h": [w_k2]}
                for n in range(NB):
                    for m in range(2):
                        p = psr.take()
                        t_ = group([lnr[n], w_r, p.free], chain(p.ap[:, :], [(Wr[:, k, m * 128:(m + 1) * 128],
                                                                              xs(n, k)) for k in range(2)]))
                        a_ = A.do([t_, s["e"]], act, sig[m], p.ap[:, :], ACT.Sigmoid, bias=b_r[:, m:m + 1])
                        p.release(a_)
                        init = 0.0 if n % 4 == 0 else rl[:, m:m + 1]
                        v_ = V.do([a_, c_half, s["rl"]], nc.vector.tensor_tensor_scan, sig[m],
                                  half[:, 0:1].broadcast_to([128, BW]), sig[m], init, ALU.mult, ALU.add)
                        l_ = V.do([v_], nc.vector.tensor_copy, rl[:, m:m + 1], sig[m][:, BW - 1:BW])
                        et = V.do([v_, l_], stt, out=e_[:, m, :], in0=sig[m], scalar=0.5, in1=xs(n, m),
                                  op0=ALU.mult, op1=ALU.add)
                    s["rl"] = l_
                    yield
                    R = []
                    yield from norm_stages(e_[:, :, :], et, h_[:, :, :], R, big, psr, (l1s, l1b), dst_free=s["h"])
                    s["e"] = R[0]
                    hr = R[0]
                    yield
                    acc = [racc.take(), racc.take()]
                    pend = None
                    for m in range(9):
                        if m < 8:
                            p = psr.take()
                            t_ = group([hr, p.free], chain(p.ap[:, :], [(W1[:, k, m * 128:(m + 1) * 128],
                                                                         h_[:, k, :]) for k in range(2)]))
                            g_ = ac.take()
                            a_ = A.do([t_, g_.free], act, g_.ap[:, :], p.ap[:, :], ACT.Gelu_apprx_tanh,
                                      bias=b1[:, m:m + 1])
                            p.release(a_)
                            yield
                        if m > 0:
                            ta = group([pend[1], acc[0].free, acc[1].free],
                                       [(acc[o].ap[:, :], W2[:, m - 1, o * 128:(o + 1) * 128], pend[0].ap[:, :],
                                         m == 1, m == 8) for o in range(2)])
                            pend[0].release(ta)
                        pend = (g_, a_)
                    for m in range(2):
                        et = V.do([ta, s["e"]], stt, out=e_[:, m, :], in0=acc[m].ap[:, :], scalar=b2[:, m:m + 1],
                                  in1=h_[:, m, :], op0=ALU.add, op1=ALU.add)
                        acc[m].release(et)
                    yield
                    R = []
                    yield from norm_stages(e_[:, :, :], et, h_[:, :, :], R, big, psr, (l2s, l2b), dst_free=[et])
                    s["e"] = R[0]
                    g_ = xw[n] = V.do([R[0], xw[n]], nvt, xT[:, :, n * BW:(n + 1) * BW], xT[:, :, n * BW:(n + 1) * BW], h_[:, :, :],
                              ALU.add)
                    s["h"] = [g_]
                    done.append(g_)
                    yield

            xa = sb("xa", [128, 2, 2, BW], F32R)
            f1 = sb("f1", [128, 2, 8, BW], F32R)
            f2 = Ring([sb(f"f2{i}", [128, 2, BW], F32R) for i in range(2)])

            def split(src, r_src, hi, lo, free):
                v_ = V.do([r_src, *free], nc.vector.tensor_copy, hi, src)
                return v_, G.do([v_], nc.gpsimd.tensor_tensor, lo, src, hi.bitcast(F32), ALU.subtract)

            def two(w, hi, lo):
                return [(w, hi), (w, lo)]

            def binary():
                s = {"xa": [], "f1": []}
                def split_x(n):
                    return split(xn[:, :, n * BW:(n + 1) * BW], lnr[n], xa[:, 0, :, :], xa[:, 1, :, :], s["xa"])[1]

                xr = split_x(0)
                for n in range(NB):
                    for m in range(8):
                        p = psb.take()
                        ms = slice(m * 128, (m + 1) * 128)
                        t_ = group([xr, w_k0, p.free], chain(p.ap[:, :], [
                            q for k in range(2) for q in two(K0[:, k, ms], xa[:, 0, k, :], xa[:, 1, k, :])]))
                        f_ = ft.take()
                        a1 = A.do([t_, c_s2, f_.free], act, f_.ap[:, :], p.ap[:, :], ACT.Relu, scale=s2[:, 0:1])
                        p.release(a1)
                        v1, g1_ = split(f_.ap[:, :], a1, f1[:, 0, m, :], f1[:, 1, m, :], s["f1"])
                        f_.release(g1_, v1)
                        if m % 2:
                            yield
                    s["xa"] = [t_]
                    if n + 1 < NB:
                        xr = split_x(n + 1)
                    acc = [bacc_.take(), bacc_.take()]
                    pend = None
                    for m in range(9):
                        if m < 8:
                            p = psb.take()
                            ms = slice(m * 128, (m + 1) * 128)
                            t_ = group([g1_, w_k1, p.free], chain(p.ap[:, :], [
                                q for k in range(8) for q in two(K1[:, k, ms], f1[:, 0, k, :], f1[:, 1, k, :])]))
                            f_, g_ = ft.take(), f2.take()
                            a1 = A.do([t_, f_.free], act, f_.ap[:, :], p.ap[:, :], ACT.Relu, scale=s2[:, 1:2])
                            p.release(a1)
                            v1, gt = split(f_.ap[:, :], a1, g_.ap[:, 0, :], g_.ap[:, 1, :], g_.free)
                            f_.release(gt, v1)
                            yield
                        if m > 0:
                            ta = group([pend[1], w_k2, acc[0].free, acc[1].free],
                                       [(acc[o].ap[:, :], K2[:, m - 1, o * 128:(o + 1) * 128], pend[0].ap[:, i, :],
                                         m == 1 and i == 0, m == 8 and i == 1) for o in range(2) for i in range(2)])
                            pend[0].release(ta)
                        pend = (g_, gt)
                    s["f1"] = [t_]
                    for m in range(2):
                        v_ = xw[n] = V.do([ta, xw[n]], stt, out=blk(xT, m, n), in0=acc[m].ap[:, :], scalar=sc[:, 2:3],
                                  in1=blk(xT, m, n), op0=ALU.mult, op1=ALU.add)
                        acc[m].release(v_)
                    fdone.append(v_)
                    yield

            interleave((reten(), 1.0), (binary(), 1.35))
            barrier()
            ph.close()
            return [[done[n], fdone[n]] for n in range(NB)]

        def layer3(ready):
            ph = ExitStack()
            sb = alloc(ph)
            WoP = sb("aWo", [128, 4, 256])
            WQ, WK = sb("WQr", [128, 2, 8, 128]), sb("WKr", [128, 2, 8, 128])
            Wvn = sb("aWv", [128, 2, 256])
            alf = sb("alf", [128, 2])
            negb = sb("negb", [128, 2, 128], BF16)
            selS = sb("selS", [128, 4, 32])
            orow = sb("orow", [1, 128 + BW], BF16)
            Pb = [sb(f"P{i}", [128, 2, BW]) for i in range(4)]
            ph2 = ExitStack()
            sb2 = alloc(ph2)
            Wqn, Wkn = sb2("aWq", [128, 2, 256]), sb2("aWk", [128, 2, 256])
            th4 = [sb2(f"th{i}", [128, 2, 256]) for i in range(4)]
            for t_, n_ in ((Wqn, "aWq"), (Wkn, "aWk"), (Wvn, "aWv")):
                w_a = dma([], "w3a", t_[:, :, :], d[n_])
            c0 = V.do([], nc.vector.memset, WoP[:, :, :], 0.0)
            for j in range(4):
                w_o = dma([c0], "w3o", WoP[32 * j:32 * j + 16, :, :], d["aWo"][:, j, :, :])
            for i, n_ in enumerate(("theta", "theta_noise", "phi", "phi_noise")):
                w_t = dma([], "w3t", th4[i][:, :, :], d[n_])
            mk = None
            mf = sb2("mf", [128, 128])[:, :]
            for i, (cm, st_) in enumerate(((1, -1), (-1, 1))):
                g_ = G.do([mk], nc.gpsimd.memset, mf, 0.0)
                g_ = G.do([g_], nc.gpsimd.affine_select, out=mf, in_=mf, compare_op=ALU.is_ge, fill=NEG, base=0,
                          pattern=[[st_, 128]], channel_multiplier=cm)
                mk = V.do([g_], nc.vector.tensor_copy, negb[:, i, :], mf)
            for i, lo in enumerate((48, 16)):
                V.do([], nc.vector.tensor_reduce, alf[:, i:i + 1],
                     ident[:, :].rearrange("p (h c) -> p h c", h=2)[:, :, lo:lo + 16], AX.XY, ALU.add, negate=True)
            V.do([], nc.vector.tensor_copy, selS[:, :, :],
                 ident[:, :].rearrange("p (j c) -> p j c", j=4)[:, :, 16:17].broadcast_to([128, 4, 32]))
            v_ = V.do([], nc.vector.memset, orow[:, :], 1.0)
            v_ = V.do([v_], nc.vector.memset, orow[:, 0:128], 0.0)
            for o_ in (32, 96):
                V.do([v_], nc.vector.memset, orow[:, o_:o_ + 1], 1.0)
            psx = Ring(PS[0:3])
            big = Ring([sb2(f"bi{i}", [128, 2, BW]) for i in range(4)])
            TR = [Pb[0][:, i, :].rearrange("p (k m) -> p k m", k=2) for i in range(2)]
            ki = sb2("ki", [128, 2, 256], I32)
            kf = sb2("kf", [128, 2, 2, 256])
            tr = []

            def weights():
                for w_, r_, sc_ in ((Wqn, WQ, 0.25), (Wkn, WK, 1.0)):
                    g_ = G.do([], nc.gpsimd.memset, r_[:, :, :, :], 0.0)
                    for o_ in (0, 16, 48):
                        for k in range(2):
                            c_rep = V.do([g_, w_a], nvs,
                                         r_[:, k, :, :].rearrange("p a (b c) -> p (a b) c", b=2)[:, :, o_:o_ + 16],
                                         w_[:, k, :].rearrange("p (h c) -> p h c", c=16), sc_, None, ALU.mult)
                        yield
                v_ = kf_ = None
                for i, (a0, b0, off) in enumerate(((0, 1, 0.25), (2, 3, 0.0))):
                    t0, t1 = th4[a0][:, :, :], th4[b0][:, :, :]
                    v_ = V.do([w_t, v_], nvt, t0, t0, t1, ALU.add)
                    yield
                    v_ = V.do([v_], nvs, t1, t0, 0.15915494309189535, off, ALU.mult, ALU.add)
                    v_ = V.do([v_], nc.vector.tensor_copy, ki[:, :, :], t1)
                    v_ = V.do([v_, kf_], nc.vector.tensor_copy, kf[:, 0, :, :], ki[:, :, :])
                    yield
                    v_ = V.do([v_], nvt, t1, t1, kf[:, 0, :, :], ALU.subtract)
                    u_ = V.do([v_], nvs, kf[:, 1, :, :], t1, -0.5, -1.0, ALU.is_lt, ALU.mult)
                    w_ = V.do([v_], nvs, t1, t1, 0.5, None, ALU.is_gt)
                    yield
                    v_ = V.do([w_, u_], nvt, t1, t1, kf[:, 1, :, :], ALU.add)
                    v_ = kf_ = V.do([v_], nvt, t1, t1, kf[:, 0, :, :], ALU.add)
                    yield
                    if off:
                        v_ = V.do([v_], nvs, t0, t0, 1.5707963267948966, None, ALU.add)
                    v_ = V.do([v_], stt, out=t0, in0=t1, scalar=-6.28125, in1=t0, op0=ALU.mult, op1=ALU.add)
                    yield
                    v_ = V.do([v_], stt, out=t0, in0=t1, scalar=-0.0019353071795864769, in1=t0, op0=ALU.mult,
                              op1=ALU.add)
                    v_ = V.do([v_], nvs, t0, t0, 3.1415925, -3.1415925, ALU.min, ALU.max)
                    c_tr = A.do([v_], act, TR[i][:, :, :], t0, ACT.Sin)
                    tr.append(c_tr)

            lnr = layer_norm_all(ready, big, psx, weights())
            c_tr = tr[-1]
            barrier()
            ph2.close()

            NQ = 4
            QS = [sb(f"QS{i}", [128, 2, SEQ], F32R) for i in range(2)]
            KS = [sb(f"KS{i}", [128, 2, SEQ], F32R) for i in range(2)]
            Va = sb("Va", [128, 16, 288])
            hi = Ring([sb(f"hi{i}", [128, BW], F32R) for i in range(2)])
            Zq = [[sb(f"zq{h}{i}", [128, BW], F32R) for i in range(2)] for h in range(2)]
            for h in range(2):
                for z in Zq[h]:
                    c_zq = V.do([], nvs, z[64 - 64 * h:128 - 64 * h, :].rearrange("p (a b) -> p a b", a=4),
                                ident[64 - 64 * h:128 - 64 * h, None, :].broadcast_to([64, 4, 128]), 0.0, None,
                                ALU.mult)
            Zr = [Ring(z) for z in Zq]
            osb, On = sb("osb", [128, BW]), sb("On", [128, BW])
            pm = sb("pm", [128, 4, 16, 4])
            mxs = sb("mxs", [128, 4, 16], BF16)
            c_pm = V.do([], nc.vector.memset, pm[:, :, :, :], -3.0e38)
            c_va = G.do([], nc.gpsimd.memset, Va[:, :, :], 1.0)
            S2 = Ring([(PS[3], PS[4]), (PS[5], PS[6])])
            po = Ring([PS[7]])
            qfree, kfree = [[], []], [[], []]
            Qr, Kr = {}, {}
            sv = {"va": [c_va], "mxs": None, "pm": [c_pm], "o": None, "on": None, "fin": None}
            xdone = {}

            def ffn():
                tmp = Ring([Pb[1 + i // 2][:, i % 2, :] for i in range(6)])
                psf = Ring(PS[3:7])
                for n in range(NB):
                    for m in range(2):
                        ms = slice(m * 128, (m + 1) * 128)
                        t2 = []
                        for i in range(2):
                            p = psf.take()
                            t_ = group([lnr[n], c_tr, p.free], chain(p.ap[:, :], [(TR[i][:, k, ms], xs(n, k))
                                                                                  for k in range(2)]))
                            s_ = tmp.take()
                            a_ = A.do([t_, s_.free], act, s_.ap[:, :], p.ap[:, :], ACT.Square)
                            p.release(a_)
                            t2.append((s_, a_))
                        (s0, a0), (s1, a1) = t2
                        yield
                        g_ = G.do([a0, a1, G.last()], nc.gpsimd.tensor_tensor, s0.ap[:, :], s0.ap[:, :], s1.ap[:, :], ALU.add)
                        s1.release(g_)
                        yield
                        a_ = A.do([g_], act, s0.ap[:, :], s0.ap[:, :], ACT.Sqrt)
                        yield
                        v_ = xw[n] = V.do([a_, xw[n]], nvt, blk(xT, m, n), blk(xT, m, n), s0.ap[:, :], ALU.add)
                        s0.release(v_)
                        yield
                sv["pfree"] = [v_, t_]

            def vproj(b):
                for kt in range(16):
                    ts = slice(b * SEQ + kt * 128, b * SEQ + (kt + 1) * 128)
                    p = psx.take()
                    t_ = group([p.free], chain(p.ap[:, 0:256], [(xn[:, k, ts], Wvn[:, k, :]) for k in range(2)]))
                    v_ = V.do([t_, *sv["va"]], nc.vector.tensor_copy,
                              Va[:, kt, 0:272].rearrange("p (h c) -> p h c", c=17)[:, :, 0:16],
                              p.ap[:, 0:256].rearrange("p (h c) -> p h c", c=16))
                    p.release(v_)
                    yield
                sv["var"] = v_

            def prep(b, g):
                i = (b * 4 + g) % 2
                sp = {}
                for W_, S_, col, fr in ((WQ, QS, 0, qfree), (WK, KS, 1, kfree)):
                    for pr in range(2):
                        for n in range(NQ):
                            bs = slice(b * SEQ + n * BW, b * SEQ + (n + 1) * BW)
                            p = psx.take()
                            mms = chain(p.ap[:, :], [(W_[:, k, 2 * g + pr, :], xn[:, k, bs]) for k in range(2)])
                            if col:
                                mms[-1] = mms[-1][:4] + (False,)
                                mms.append((p.ap[:, :], orow[:, 0:128], orow[:, 128:128 + BW], False, True))
                            t_ = group([p.free], mms)
                            h_ = hi.take()
                            a_ = A.do([t_, h_.free], act, h_.ap[:, :], p.ap[:, :], ACT.Copy)
                            s_ = V.do([a_, *fr[i]], stt, out=S_[i][:, pr, n * BW:(n + 1) * BW],
                                      in0=h_.ap[:, :].bitcast(F32), scalar=alf[:, col:col + 1], in1=p.ap[:, :],
                                      op0=ALU.mult, op1=ALU.add)
                            h_.release(s_)
                            p.release(s_)
                            sp[(col, pr, n)] = s_
                            yield
                Q, K = QS[i], KS[i]

                def padded(hd, n):
                    pr, r0 = hd // 2, 64 * (hd % 2)
                    z = Zr[hd % 2].take()
                    z.tok = G.do([sp[(0, pr, n)], G.last(), c_zq, z.free], nc.gpsimd.tensor_copy, z.ap[r0:r0 + 64, :],
                                 Q[r0:r0 + 64, pr, n * BW:(n + 1) * BW])
                    return z

                def place(pr):
                    v_ = sv["pmw"]
                    m_ = V.do([v_, sv["mxs"]], nc.vector.tensor_reduce, mxs[:, 2 * pr:2 * pr + 2, :],
                              pm[:, 2 * pr:2 * pr + 2, :, :], AX.X, ALU.max, negate=True)
                    sv["pm"] = [m_]
                    for n in range(NQ):
                        p = psx.take()
                        mms = [(p.ap[32 + 64 * hh:33 + 64 * hh, c * 128:(c + 1) * 128],
                                mxs[:, 2 * pr + hh, 4 * n + c:4 * n + c + 1], identb[:, :], True, True)
                               for hh in range(2) for c in range(4)]
                        t_ = group([m_, p.free], mms)
                        q_ = A.do([t_], act, Q[32:33, pr, n * BW:(n + 1) * BW], p.ap[32:33, :], ACT.Copy)
                        v_ = V.do([t_], nc.vector.tensor_copy, Q[96:97, pr, n * BW:(n + 1) * BW], p.ap[96:97, :])
                        p.release(q_, v_)
                        yield
                    sv["mxs"] = t_
                    Qr[(b, g)] = [q_, v_]

                steps = [(hd, n) for hd in range(4) for n in range(NQ)]
                zs = padded(*steps[0])
                for j, (hd, n) in enumerate(steps):
                    pr = hd // 2
                    z = zs
                    if j + 1 < len(steps):
                        zs = padded(*steps[j + 1])
                    for qt in range(4 * n, 4 * n + 4):
                        q0 = (qt - 4 * n) * 128
                        for c in range(n + 1):
                            w = min(512, (qt + 1) * 128 - c * 512)
                            p = psx.take()
                            mms = [(p.ap[:, 0:w], z.ap[:, q0:q0 + 128], K[:, pr, c * 512:c * 512 + w], True, c < n)]
                            if c == n:
                                mms.append((p.ap[:, w - 128:w], identb[:, :], negb[:, 0, :], False, True))
                            t_ = group([sp[(1, pr, c)], z.tok, p.free], mms)
                            v_ = V.do([t_, *sv["pm"]], nc.vector.tensor_reduce, pm[:, hd, qt, c:c + 1],
                                      p.ap[:, 0:w], AX.X, ALU.max)
                            p.release(v_)
                            yield
                    z.release(t_)
                    sv["pmw"] = v_
                    if j == 9:
                        yield from place(0)
                yield from place(1)

            def main(b, g):
                i = (b * 4 + g) % 2
                Q, K = QS[i], KS[i]
                for n in range(NQ):
                    o_ = po.take()
                    nk = 4 * n + 4
                    pend = None
                    for kt in range(nk):
                        if kt < nk:
                            off = max(0, (kt - 4 * n) * 128)
                            cur = []
                            for pr in range(2):
                                s2, P_ = S2.take(), Pr.take()
                                mms = []
                                for hh in range(2):
                                    rs = slice(64 * hh, 64 * hh + 64)
                                    diag = kt >= 4 * n
                                    mms.append((s2.ap[hh][:, off:BW], K[rs, pr, kt * 128:(kt + 1) * 128],
                                                Q[rs, pr, n * BW + off:(n + 1) * BW], True, not diag))
                                if diag:
                                    for hh in range(2):
                                        mms.append((s2.ap[hh][:, off:off + 128], identb[:, :], negb[:, 1, :], False,
                                                    True))
                                t_ = group([Qr[(b, g)], s2.free], mms)
                                for hh in range(2):
                                    a_ = A.do([t_, P_.free], act, P_.ap[:, hh, off:BW], s2.ap[hh][:, off:BW],
                                              ACT.Exp)
                                s2.release(a_)
                                cur.append((P_, a_))
                                yield
                                step()
                                if pr == 1 and pend is not None:
                                    tp = pv(g, pend, o_, nk)
                                    pend = None
                                    yield
                            pend = (kt, off, cur)
                    yield
                    tp = pv(g, pend, o_, nk)
                    drain()
                    a_ = A.do([tp, sv["o"]], act, osb[:, :], o_.ap[:, :], ACT.Copy)
                    o_.release(a_)
                    sv["fin"] = finish(b, g, n, a_)
                    yield
                qfree[i] = kfree[i] = [tp]
                sv["va"] = [tp]

            def finish(b, g, n, a_):
                p = psx.take()
                t_ = group([a_, p.free], [(p.ap[:, :], selS[:, :, :].rearrange("p a b -> p (a b)"), osb[:, :], True,
                                           True)])
                yield
                for c in range(4):
                    cs = slice(c * 128, (c + 1) * 128)
                    v_ = V.do([t_, sv["on"]], nc.vector.reciprocal, On[:, cs], p.ap[:, cs])
                    v_ = V.do([v_], nvt, On[:, cs], On[:, cs], osb[:, cs], ALU.mult)
                    if c < 3:
                        yield
                p.release(v_)
                sv["o"] = v_
                yield
                bs = slice(b * SEQ + n * BW, b * SEQ + (n + 1) * BW)
                for m in range(2):
                    p = psx.take()
                    t_ = group([v_, p.free], [(p.ap[:, :], WoP[:, g, m * 128:(m + 1) * 128], On[:, :], True, True)])
                    x_ = xw[4 * b + n] = V.do([t_, xw[4 * b + n]], nvt, xT[:, m, bs], xT[:, m, bs], p.ap[:, :],
                                              ALU.add)
                    p.release(x_)
                    sv["on"] = t_
                    yield
                xdone[4 * b + n] = x_

            def drain():
                if sv["fin"] is not None:
                    for _ in sv["fin"]:
                        pass
                sv["fin"] = None

            def step():
                if sv["fin"] is not None:
                    next(sv["fin"], None)

            def pv(g, pend, o_, nk):
                kt, off, cur = pend
                mms = []
                for hd in range(4):
                    P_ = cur[hd // 2][0]
                    h = 4 * g + hd
                    mms.append((o_.ap[32 * hd:32 * hd + 32, off:BW], Va[:, kt, h * 17:h * 17 + 32],
                                P_.ap[:, hd % 2, off:BW], kt == 0, kt == nk - 1))
                tp = group([cur[0][1], cur[1][1], sv["var"]] + (o_.free if kt == 0 else []), mms)
                for P_, _ in cur:
                    P_.release(tp)
                return tp

            order = [(b, g) for b in range(2) for g in range(4)]
            def first():
                yield from vproj(0)
                yield from prep(0, 0)

            interleave((first(), 1.0), (ffn(), 3.0))
            Pr = Ring(Pb)
            Pr.free = [list(sv["pfree"]) for _ in Pb]
            S2.free = [list(sv["pfree"]) for _ in range(2)]
            for j, (b, g) in enumerate(order):
                if (b, g) == (1, 0):
                    for _ in vproj(1):
                        pass
                if j + 1 < len(order):
                    interleave((main(b, g), 1.45), (prep(*order[j + 1]), 1.0))
                else:
                    for _ in main(b, g):
                        pass
            drain()
            ph.close()
            return [xdone[n] for n in range(NB)]

        ready = xload
        ready = layer0(ready)
        ready = layer1(ready)
        ready = layer2(ready)
        ready = layer3(ready)
        for n in range(NB):
            tok = dma([ready[n]], "out", out[:, :, n * BW:(n + 1) * BW], xT[:, :, n * BW:(n + 1) * BW])
        SP.wait(tok)

        block = ctx.enter_context(nc.Block())

        @block.sync
        def _(eng):
            SP.emit(eng)

        @block.tensor
        def _(eng):
            PE.emit(eng)

        @block.vector
        def _(eng):
            V.emit(eng)

        @block.scalar
        def _(eng):
            A.emit(eng)

        @block.gpsimd
        def _(eng):
            G.emit(eng)


def layout(i):
    import numpy as np

    def c(a):
        return np.ascontiguousarray(a)

    def wt(a):
        return c(a.reshape(-1, 128, a.shape[-1]).transpose(1, 0, 2))

    def pv(*vs):
        cols = [v.reshape(-1, 128).T for v in vs]
        n = sum(x.shape[1] for x in cols)
        return cols, n

    def vec(width, *vs):
        cols, n = pv(*vs)
        cols.append(np.zeros((128, width - n), np.float32))
        return c(np.concatenate(cols, axis=1))

    def ex(a):
        e, k, o = a.shape
        return c(a.reshape(e, k // 128, 128, o).transpose(2, 0, 1, 3))

    g = {k: np.asarray(v) for k, v in i.items()}
    r = {}
    r["x"] = c(g["L0_attn_x"].reshape(T, 2, 128).transpose(2, 1, 0))
    for n, s in (("Wq", "L0_attn_Wq"), ("Wk", "L0_attn_Wk"), ("Wv", "L0_attn_Wv"), ("Wg", "L0_attn_Wg"),
                 ("Wgk1", "L0_attn_Wgk1"), ("Wo", "L0_attn_Wo"), ("Wr", "L0_ffn_Wr"), ("mWi", "L1_attn_W_in"),
                 ("mWd", "L1_attn_Wd"), ("mWo", "L1_attn_W_out"), ("rWr", "L2_attn_W_ret"), ("rW1", "L2_attn_W1"),
                 ("rW2", "L2_attn_W2"), ("theta", "L3_ffn_theta"), ("theta_noise", "L3_ffn_theta_noise"),
                 ("phi", "L3_ffn_phi"), ("phi_noise", "L3_ffn_phi_noise")):
        r[n] = wt(g[s])
    r["Wgk2"] = c(g["L0_attn_Wgk2"])
    r["vec0"] = vec(3, g["L0_attn_bgk2"], g["L0_attn_g_norm_weight"])
    r["F1"], r["F3"], r["F2"] = ex(g["L0_ffn_W1"]), ex(g["L0_ffn_W3"]), ex(g["L0_ffn_W2"])
    r["vec1"] = vec(32, g["L1_attn_ln_gamma"], g["L1_attn_ln_beta"], g["L1_attn_conv_b"], g["L1_attn_bd"],
                    g["L1_attn_D_vec"])
    r["mcw"] = c(g["L1_attn_conv_w"].reshape(4, 128, 4).transpose(1, 0, 2))
    r["mA"] = c(g["L1_attn_A_log"].reshape(16, 1))
    r["mB"] = wt(c(g["L1_attn_B_mat"].T))
    r["mC"] = c(g["L1_attn_C_mat"].T)
    r["pWq"] = c(g["L1_ffn_Wq"].reshape(16, 128, 256).transpose(1, 0, 2))
    r["keys"] = c(g["L1_ffn_keys"].transpose(3, 2, 0, 1).reshape(128, 16, 128))
    r["pWi"] = wt(c(g["L1_ffn_W_in"].T))
    r["pWo"] = wt(c(g["L1_ffn_W_out"].T))
    r["tab0"] = c(np.concatenate([g["L1_ffn_in_a"], g["L1_ffn_in_b"]], axis=1))
    r["tab1"] = c(np.concatenate([g["L1_ffn_out_a"], g["L1_ffn_out_b"]], axis=1))
    sc = [np.broadcast_to(g[f"L2_ffn_s{n}"], (128,)) for n in range(3)]
    r["vec2"] = vec(32, g["L2_attn_b_ret"], g["L2_attn_ln1_scale"], g["L2_attn_ln1_bias"], g["L2_attn_ln2_scale"],
                    g["L2_attn_ln2_bias"], g["L2_attn_b1"], g["L2_attn_b2"], *sc)
    for n in ("k0", "k1", "k2"):
        r[n] = wt(g[f"L2_ffn_{n}"])
    r["k2"] = r["k2"].reshape(128, -1)
    for n, s in (("aWq", "q"), ("aWk", "k"), ("aWv", "v")):
        r[n] = wt(c(g[f"L3_attn_{s}_proj_weight"].T))
    r["aWo"] = c(g["L3_attn_o_proj_weight"].T.reshape(4, 4, 16, 256).transpose(2, 1, 0, 3))
    return r


def kernel(**inputs):
    import numpy as np
    import concourse.bacc as bacc
    from concourse.bass_utils import run_bass_kernel_spmd

    arrays = layout(inputs)
    nc = bacc.Bacc("TRN2", target_bir_lowering=False, num_devices=1)
    d = {n: nc.dram_tensor(f"in_{n}", a.shape, mybir.dt.from_np(a.dtype), kind="ExternalInput").ap()
         for n, a in arrays.items()}
    out = nc.dram_tensor("out_0", (128, 2, T), F32, kind="ExternalOutput").ap()
    build(nc, d, out)
    r = run_bass_kernel_spmd(nc, [{f"in_{n}": a for n, a in arrays.items()}], core_ids=[0])
    y = r.results[0]["out_0"]
    return np.ascontiguousarray(y.transpose(2, 1, 0)).reshape(2, SEQ, 256)
```
